# Optimizing a Trainium2 kernel written in Bass

```python
import numpy as np
import jax
import jax.numpy as jnp

def _softmax(x, axis=-1):
    return jax.nn.softmax(x, axis=axis)

def _gelu(x):
    return jax.nn.gelu(x, approximate=True)

def _silu(x):
    return jax.nn.silu(x)

def _sigmoid(x):
    return jax.nn.sigmoid(x)

def _layernorm(x, axis=-1, eps=1e-05):
    m = jnp.mean(x, axis=axis, keepdims=True)
    v = jnp.var(x, axis=axis, keepdims=True)
    return (x - m) / jnp.sqrt(v + eps)

def _scatter_add(tgt, idx, src, axis=0):
    return tgt.at[idx].add(src)

def _segment_sum(src, seg, n):
    return jax.ops.segment_sum(src, seg, n)
kernel_name = 'mk_cond_seq_d4_seqx_r8_1734e7'

def setup_inputs(seed: int=0):
    np.random.seed(seed)
    _w = jnp.asarray

    def _rec_inputs():
        import jax
        import jax.numpy as jnp
        _rk = jax.random.key(seed)
        x = 0.5 + 0.2887 * jax.random.normal(jax.random.fold_in(_rk, 1), (64, 32, 256), jnp.float32)
        _lenS = 32 - jax.random.randint(jax.random.fold_in(_rk, 7), (64,), 0, max(1, 32 // 4) + 1, jnp.int32)
        _lenS2 = 32 - jax.random.randint(jax.random.fold_in(_rk, 8), (64,), 0, max(1, 32 // 4) + 1, jnp.int32)
        itok_B_17_1546 = jax.random.randint(jax.random.fold_in(_rk, 12), (64,), 17, 1547, jnp.int32)
        itok_B_1_2 = jax.random.randint(jax.random.fold_in(_rk, 13), (64,), 1, 3, jnp.int32)
        return (x, itok_B_17_1546, itok_B_1_2, _lenS)
    x, itok_B_17_1546, itok_B_1_2, _lenS = _rec_inputs()

    def _L0_cond_setup():
        import jax, jax.numpy as jnp
        import numpy as np
        B, T, V = (8, 64, 256)
        H = 4 * V
        key = jax.random.key(seed)
        ks = jax.random.split(key, 16)
        s = lambda n: 1.0 / np.sqrt(n)
        inp = {'x': jax.random.uniform(ks[0], (B, T, V), dtype=jnp.float32), 'lens': jax.random.randint(ks[1], (B,), 1, T, dtype=jnp.int64), 'target_codes': jax.random.randint(ks[2], (B,), 0, V, dtype=jnp.int64), 'Wq': jax.random.normal(ks[3], (V, V), jnp.float32) * s(V), 'Wk': jax.random.normal(ks[4], (V, V), jnp.float32) * s(V), 'Wv': jax.random.normal(ks[5], (V, V), jnp.float32) * s(V), 'Wp': jax.random.normal(ks[6], (V, V), jnp.float32) * s(V), 'bp': jnp.zeros((V,), jnp.float32), 'cW1': jax.random.normal(ks[7], (V, H), jnp.float32) * s(V), 'cb1': jnp.zeros((H,), jnp.float32), 'cW2': jax.random.normal(ks[8], (H, V), jnp.float32) * s(H), 'cb2': jnp.zeros((V,), jnp.float32), 'mW1': jax.random.normal(ks[9], (2 * V, H), jnp.float32) * s(2 * V), 'mb1': jnp.zeros((H,), jnp.float32), 'mW2': jax.random.normal(ks[10], (H, V), jnp.float32) * s(H), 'mb2': jnp.zeros((V,), jnp.float32)}
        return inp
    _L0_cond_all = _L0_cond_setup()
    _L0_cond_in = {k: v for k, v in _L0_cond_all.items() if k in ('Wq', 'Wk', 'Wv', 'Wp', 'bp', 'cW1', 'cb1', 'cW2', 'cb2', 'mW1', 'mb1', 'mW2', 'mb2')}
    del _L0_cond_all

    def _L1_cond_setup():
        import jax, jax.numpy as jnp
        import numpy as np
        H = 256
        K = 128
        R = 3
        B = 8
        S = 256
        LN_EPS = 1e-05
        key = jax.random.key(seed)
        ks = jax.random.split(key, 8)
        sd_d = 1.0 / np.sqrt(H)
        sd_u = 1.0 / np.sqrt(K)
        return {'role': jax.random.randint(ks[0], (B,), 0, R), 'hidden_states': jax.random.normal(ks[1], (B, S, H), dtype=jnp.float32), 'W_down': jax.random.uniform(ks[2], (R, H, K), jnp.float32, -sd_d, sd_d), 'b_down': jax.random.uniform(ks[3], (R, K), jnp.float32, -sd_d, sd_d), 'W_up': jax.random.uniform(ks[4], (R, K, H), jnp.float32, -sd_u, sd_u), 'b_up': jax.random.uniform(ks[5], (R, H), jnp.float32, -sd_u, sd_u), 'gamma': jnp.ones((R, H), jnp.float32), 'beta': jnp.zeros((R, H), jnp.float32)}
    _L1_cond_all = _L1_cond_setup()
    _L1_cond_in = {k: v for k, v in _L1_cond_all.items() if k in ('W_down', 'b_down', 'W_up', 'b_up', 'gamma', 'beta')}
    del _L1_cond_all

    def _L2_cond_setup():
        import jax, jax.numpy as jnp
        import numpy as np
        B, S, H = (8, 256, 256)
        BN = 128
        E = 3
        LN_EPS = 1e-05
        key = jax.random.key(seed)
        ks = jax.random.split(key, 8)
        stream = jax.random.randint(ks[0], (B,), 0, E, dtype=jnp.int32)
        hidden_states = jax.random.normal(ks[1], (B, S, H), dtype=jnp.float32)
        W_down = jax.random.normal(ks[2], (E, H, BN), dtype=jnp.float32) * 0.02
        b_down = jnp.zeros((E, BN), dtype=jnp.float32)
        W_up = jax.random.normal(ks[3], (E, BN, H), dtype=jnp.float32) * 0.02
        b_up = jnp.zeros((E, H), dtype=jnp.float32)
        ln_w = jnp.ones((E, H), dtype=jnp.float32)
        ln_b = jnp.zeros((E, H), dtype=jnp.float32)
        return {'stream': stream, 'hidden_states': hidden_states, 'W_down': W_down, 'b_down': b_down, 'W_up': W_up, 'b_up': b_up, 'ln_w': ln_w, 'ln_b': ln_b}
    _L2_cond_all = _L2_cond_setup()
    _L2_cond_in = {k: v for k, v in _L2_cond_all.items() if k in ('W_down', 'b_down', 'W_up', 'b_up', 'ln_w', 'ln_b')}
    del _L2_cond_all

    def _L3_cond_setup():
        import jax, jax.numpy as jnp
        import numpy as np
        B, S, H = (8, 256, 256)
        BN = 128
        E = 3
        LN_EPS = 1e-05
        key = jax.random.key(seed)
        ks = jax.random.split(key, 8)
        stream = jax.random.randint(ks[0], (B,), 0, E, dtype=jnp.int32)
        hidden_states = jax.random.normal(ks[1], (B, S, H), dtype=jnp.float32)
        W_down = jax.random.normal(ks[2], (E, H, BN), dtype=jnp.float32) * 0.02
        b_down = jnp.zeros((E, BN), dtype=jnp.float32)
        W_up = jax.random.normal(ks[3], (E, BN, H), dtype=jnp.float32) * 0.02
        b_up = jnp.zeros((E, H), dtype=jnp.float32)
        ln_w = jnp.ones((E, H), dtype=jnp.float32)
        ln_b = jnp.zeros((E, H), dtype=jnp.float32)
        return {'stream': stream, 'hidden_states': hidden_states, 'W_down': W_down, 'b_down': b_down, 'W_up': W_up, 'b_up': b_up, 'ln_w': ln_w, 'ln_b': ln_b}
    _L3_cond_all = _L3_cond_setup()
    _L3_cond_in = {k: v for k, v in _L3_cond_all.items() if k in ('W_down', 'b_down', 'W_up', 'b_up', 'ln_w', 'ln_b')}
    del _L3_cond_all
    return {'x': x, 'itok_B_17_1546': itok_B_17_1546, 'itok_B_1_2': itok_B_1_2, '_lenS': _lenS, 'L0_cond_Wq': _L0_cond_in['Wq'], 'L0_cond_Wk': _L0_cond_in['Wk'], 'L0_cond_Wv': _L0_cond_in['Wv'], 'L0_cond_Wp': _L0_cond_in['Wp'], 'L0_cond_bp': _L0_cond_in['bp'], 'L0_cond_cW1': _L0_cond_in['cW1'], 'L0_cond_cb1': _L0_cond_in['cb1'], 'L0_cond_cW2': _L0_cond_in['cW2'], 'L0_cond_cb2': _L0_cond_in['cb2'], 'L0_cond_mW1': _L0_cond_in['mW1'], 'L0_cond_mb1': _L0_cond_in['mb1'], 'L0_cond_mW2': _L0_cond_in['mW2'], 'L0_cond_mb2': _L0_cond_in['mb2'], 'L1_cond_W_down': _L1_cond_in['W_down'], 'L1_cond_b_down': _L1_cond_in['b_down'], 'L1_cond_W_up': _L1_cond_in['W_up'], 'L1_cond_b_up': _L1_cond_in['b_up'], 'L1_cond_gamma': _L1_cond_in['gamma'], 'L1_cond_beta': _L1_cond_in['beta'], 'L2_cond_W_down': _L2_cond_in['W_down'], 'L2_cond_b_down': _L2_cond_in['b_down'], 'L2_cond_W_up': _L2_cond_in['W_up'], 'L2_cond_b_up': _L2_cond_in['b_up'], 'L2_cond_ln_w': _L2_cond_in['ln_w'], 'L2_cond_ln_b': _L2_cond_in['ln_b'], 'L3_cond_W_down': _L3_cond_in['W_down'], 'L3_cond_b_down': _L3_cond_in['b_down'], 'L3_cond_W_up': _L3_cond_in['W_up'], 'L3_cond_b_up': _L3_cond_in['b_up'], 'L3_cond_ln_w': _L3_cond_in['ln_w'], 'L3_cond_ln_b': _L3_cond_in['ln_b']}

def reference(x, itok_B_17_1546, itok_B_1_2, _lenS, L0_cond_Wq, L0_cond_Wk, L0_cond_Wv, L0_cond_Wp, L0_cond_bp, L0_cond_cW1, L0_cond_cb1, L0_cond_cW2, L0_cond_cb2, L0_cond_mW1, L0_cond_mb1, L0_cond_mW2, L0_cond_mb2, L1_cond_W_down, L1_cond_b_down, L1_cond_W_up, L1_cond_b_up, L1_cond_gamma, L1_cond_beta, L2_cond_W_down, L2_cond_b_down, L2_cond_W_up, L2_cond_b_up, L2_cond_ln_w, L2_cond_ln_b, L3_cond_W_down, L3_cond_b_down, L3_cond_W_up, L3_cond_b_up, L3_cond_ln_w, L3_cond_ln_b):
    import jax
    import jax.numpy as jnp

    def _L0_cond_ref(x, lens, target_codes, Wq, Wk, Wv, Wp, bp, cW1, cb1, cW2, cb2, mW1, mb1, mW2, mb2):
        import jax, jax.numpy as jnp
        import numpy as np
        B, T, V = (8, 64, 256)
        H = 4 * V
        scale = V ** (-0.5)
        q = x @ Wq
        k = x @ Wk
        v = x @ Wv
        attn = jnp.einsum('btd,bTd->btT', q, k) * scale
        attn = jax.nn.softmax(attn, axis=-1)
        attn_out = jnp.einsum('btT,bTd->btd', attn, v) @ Wp + bp
        target_embed = jax.nn.one_hot(target_codes, V, dtype=x.dtype)[:, None, :]
        cms_out = jax.nn.gelu(attn_out @ cW1 + cb1, approximate=False) @ cW2 + cb2
        cms_out = cms_out + target_embed
        concat = jnp.concatenate([attn_out, cms_out], axis=-1)
        modifier = jax.nn.gelu(concat @ mW1 + mb1, approximate=False) @ mW2 + mb2
        out = jnp.clip(x + cms_out + modifier, 0.0, 1.0)
        return out

    def _L1_cond_ref(role, hidden_states, W_down, b_down, W_up, b_up, gamma, beta):
        import jax, jax.numpy as jnp
        import numpy as np
        H = 256
        K = 128
        R = 3
        B = 8
        S = 256
        LN_EPS = 1e-05
        h = jnp.einsum('bsh,bhk->bsk', hidden_states, W_down[role]) + b_down[role][:, None, :]
        h = jax.nn.gelu(h, approximate=False)
        u = jnp.einsum('bsk,bkh->bsh', h, W_up[role]) + b_up[role][:, None, :]
        y = hidden_states + u
        mean = jnp.mean(y, axis=-1, keepdims=True)
        var = jnp.mean(jnp.square(y - mean), axis=-1, keepdims=True)
        yn = (y - mean) * jax.lax.rsqrt(var + LN_EPS)
        return yn * gamma[role][:, None, :] + beta[role][:, None, :]

    def _L2_cond_ref(stream, hidden_states, W_down, b_down, W_up, b_up, ln_w, ln_b):
        import jax, jax.numpy as jnp
        import numpy as np
        B, S, H = (8, 256, 256)
        BN = 128
        E = 3
        LN_EPS = 1e-05
        Wd = W_down[stream]
        bd = b_down[stream]
        Wu = W_up[stream]
        bu = b_up[stream]
        g = ln_w[stream]
        b = ln_b[stream]
        residual = hidden_states
        h = jnp.einsum('bsh,bhk->bsk', hidden_states, Wd) + bd[:, None, :]
        h = jax.nn.gelu(h, approximate=False)
        h = jnp.einsum('bsk,bkh->bsh', h, Wu) + bu[:, None, :]
        h = residual + h
        mean = jnp.mean(h, axis=-1, keepdims=True)
        var = jnp.mean(jnp.square(h - mean), axis=-1, keepdims=True)
        h = (h - mean) * jax.lax.rsqrt(var + LN_EPS)
        return h * g[:, None, :] + b[:, None, :]

    def _L3_cond_ref(stream, hidden_states, W_down, b_down, W_up, b_up, ln_w, ln_b):
        import jax, jax.numpy as jnp
        import numpy as np
        B, S, H = (8, 256, 256)
        BN = 128
        E = 3
        LN_EPS = 1e-05
        Wd = W_down[stream]
        bd = b_down[stream]
        Wu = W_up[stream]
        bu = b_up[stream]
        g = ln_w[stream]
        b = ln_b[stream]
        residual = hidden_states
        h = jnp.einsum('bsh,bhk->bsk', hidden_states, Wd) + bd[:, None, :]
        h = jax.nn.gelu(h, approximate=False)
        h = jnp.einsum('bsk,bkh->bsh', h, Wu) + bu[:, None, :]
        h = residual + h
        mean = jnp.mean(h, axis=-1, keepdims=True)
        var = jnp.mean(jnp.square(h - mean), axis=-1, keepdims=True)
        h = (h - mean) * jax.lax.rsqrt(var + LN_EPS)
        return h * g[:, None, :] + b[:, None, :]
    x = _L0_cond_ref(x, _lenS, itok_B_17_1546, L0_cond_Wq, L0_cond_Wk, L0_cond_Wv, L0_cond_Wp, L0_cond_bp, L0_cond_cW1, L0_cond_cb1, L0_cond_cW2, L0_cond_cb2, L0_cond_mW1, L0_cond_mb1, L0_cond_mW2, L0_cond_mb2)
    x = _L1_cond_ref(itok_B_1_2, x, L1_cond_W_down, L1_cond_b_down, L1_cond_W_up, L1_cond_b_up, L1_cond_gamma, L1_cond_beta)
    x = _L2_cond_ref(itok_B_1_2, x, L2_cond_W_down, L2_cond_b_down, L2_cond_W_up, L2_cond_b_up, L2_cond_ln_w, L2_cond_ln_b)
    x = _L3_cond_ref(itok_B_1_2, x, L3_cond_W_down, L3_cond_b_down, L3_cond_W_up, L3_cond_b_up, L3_cond_ln_w, L3_cond_ln_b)
    return x

_drawn_inputs = setup_inputs


def setup_inputs(seed=0):
    import zlib

    import numpy as np

    out = dict(_drawn_inputs(seed))
    spreads = {'L0_cond_bp': (0.0, 0.1),
     'L0_cond_cb1': (0.0, 0.1),
     'L0_cond_cb2': (0.0, 0.1),
     'L0_cond_mb1': (0.0, 0.1),
     'L0_cond_mb2': (0.0, 0.1),
     'L1_cond_gamma': (1.0, 0.2),
     'L1_cond_beta': (0.0, 0.1),
     'L2_cond_b_down': (0.0, 0.659),
     'L2_cond_b_up': (0.0, 0.1),
     'L2_cond_ln_w': (1.0, 0.2),
     'L2_cond_ln_b': (0.0, 0.1),
     'L3_cond_b_down': (0.0, 0.722),
     'L3_cond_b_up': (0.0, 0.1),
     'L3_cond_ln_w': (1.0, 0.2),
     'L3_cond_ln_b': (0.0, 0.1)}
    factors = {'L0_cond_Wq': 4.048, 'L0_cond_Wk': 3.792}
    for name, (base, spread) in spreads.items():
        noise = np.random.default_rng([zlib.crc32(name.encode()), seed]).standard_normal(out[name].shape)
        drawn = base * np.exp(spread * noise) if base else spread * noise
        out[name] = jnp.asarray(drawn.astype(out[name].dtype))
    for name, factor in factors.items():
        out[name] = (out[name] * factor).astype(out[name].dtype)
    return out
```

```python
from contextlib import ExitStack

import concourse.bass as bass
from concourse import mybir

F32 = mybir.dt.float32
F32R = mybir.dt.float32r
I32 = mybir.dt.int32
ALU = mybir.AluOpType
ACT = mybir.ActivationFunctionType
AX = mybir.AxisListType

P = 128
B, T, V = 64, 32, 256
H = 4 * V
KD = 128
ROLES, LAYERS = 3, 3
VB = V // P
HB = H // P
Q = P // T
GT = 4
GR = GT * P
GB = GT * Q
NG = B // GB
WIN = 8
WR = WIN * T
WT = WR // P
NW = B // WIN + ROLES - 1
EPS = 1e-5
OUT_OF_RANGE = 4096

CW1, CW2, MW1, MW2 = 0, 2 * H, 4 * H, 8 * H
CHUNK = 1024
NCHUNK = 10


def build(nc, x, codes, roles, Wq, Wk, Wv, Wp, bp, cW1, cb1, cW2, cb2, mW1, mb1, mW2, mb2, adapters, out):
    x_rows = x.rearrange("b t v -> (b t) v")
    out_rows = out.rearrange("b t v -> (b t) v")

    with ExitStack() as ctx:
        def sb(name, shape, dt=F32, scope=ctx):
            return scope.enter_context(nc.sbuf_tensor(name, shape, dt))

        def sem(name):
            return ctx.enter_context(nc.semaphore(name))

        bank = [ctx.enter_context(nc.psum_tensor(f"bank{i}", [P, GR], F32)) for i in range(8)]

        ident = sb("ident", [P, P])
        ones = sb("ones", [B, P])
        batch_id = sb("batch_id", [P, B])
        feature_id = sb("feature_id", [P, VB])
        row_in_batch = sb("row_in_batch", [P, 1])
        window_id = sb("window_id", [P, NW])
        window_start8 = sb("window_start8", [P, WIN])
        slot_off = sb("slot_off", [P, WT])
        roles_i = sb("roles_i", [P, B], I32)
        role_col_i = sb("role_col_i", [B, 1], I32)
        code_col_i = sb("code_col_i", [B, 1], I32)
        row_idx = sb("row_idx", [P, NG * GT], I32)
        out_idx = sb("out_idx", [P, NW, WT], I32)
        window_meta = sb("window_meta", [P, 2, NW], I32)
        cms_bias = sb("cms_bias", [P, VB, B])
        bias_rows = sb("bias_rows", [22, P])
        bias = sb("bias", [P, 22])
        CONSTS = 6 + 2 * Q
        CB1, MB1, BP, CB2, MB2 = 0, 8, 16, 18, 20

        w_hi = sb("w_hi", [P, NCHUNK * CHUNK], F32R)
        w_lo = sb("w_lo", [P, NCHUNK * CHUNK], F32R)
        a_hi = sb("a_hi", [P, 2, VB, V], F32R)
        a_lo = sb("a_lo", [P, 2, VB, V], F32R)
        xT = sb("xT", [P, VB, NG * GR])
        at_hi = sb("at_hi", [P, VB, NG * GR], F32R)
        at_lo = sb("at_lo", [P, VB, NG * GR], F32R)

        with ExitStack() as scope:
            stage = sb("stage", [P, 2, CHUNK], scope=scope)
            raw = sb("raw", [P, 4, VB, V], scope=scope)
            wT = sb("wT", [P, 3, VB, V], scope=scope)
            rt = sb("rt", [P, 4, B], scope=scope)
            rc = sb("rc", [B, 8], scope=scope)
            rs = sb("rs", [P, 32], scope=scope)
            rw = sb("rw", [P, 10, NW * WT], scope=scope)
            pick = sb("pick", [P, NW * WT, B], scope=scope)
        with ExitStack() as scope:
            xr = sb("xr", [P, 2, GT, V], scope=scope)
            xr_hi = sb("xr_hi", [P, GT, V], F32R, scope)
            xr_lo = sb("xr_lo", [P, GT, V], F32R, scope)
            xg_hi = sb("xg_hi", [P, VB, GR], F32R, scope)
            xg_lo = sb("xg_lo", [P, VB, GR], F32R, scope)
            yz_hi = sb("yz_hi", [P, VB, GR], F32R, scope)
            yz_lo = sb("yz_lo", [P, VB, GR], F32R, scope)
            pd_hi = sb("pd_hi", [P, GT, P], F32R, scope)
            pd_lo = sb("pd_lo", [P, GT, P], F32R, scope)
            row_max = sb("row_max", [P, GT], scope=scope)
            shifted = sb("shifted", [P, GT, T], scope=scope)
            expd = sb("expd", [P, GT, T], scope=scope)
            row_sum = sb("row_sum", [P, 2, GT], scope=scope)
            prob = sb("prob", [P, GT, T], scope=scope)
            probT = sb("probT", [P, GT, T], scope=scope)
        with ExitStack() as scope:
            h_full = sb("h_full", [P, 2, GR], scope=scope)
            h_hi = sb("h_hi", [P, 4, GR], F32R, scope)
            h_lo = sb("h_lo", [P, 4, GR], F32R, scope)
            cms = sb("cms", [P, VB, GR], scope=scope)
            cms_hi = sb("cms_hi", [P, VB, GR], F32R, scope)
            cms_lo = sb("cms_lo", [P, VB, GR], F32R, scope)
        with ExitStack() as scope:
            aw = sb("aw", [P, 2, LAYERS, 2 * V], scope=scope)
            ap_ = sb("ap_", [P, 2, LAYERS, 3, V], scope=scope)
            abd = sb("abd", [P, 2, LAYERS], scope=scope)
            xw = sb("xw", [P, VB, WR], scope=scope)
            xb = sb("xb", [P, WT, V], scope=scope)
            hw = sb("hw", [P, WR], scope=scope)
            yw = sb("yw", [P, WT, V], scope=scope)
            xn = sb("xn", [P, WT, V], scope=scope)
            stats = sb("stats", [P, WT, 6], scope=scope)
            moments = sb("moments", [P, WT, 2], scope=scope)
            var_eps = sb("var_eps", [P, WT], scope=scope)
            rstd = sb("rstd", [P, WT], scope=scope)
            idx_now = sb("idx_now", [P, WT], I32, scope)
            minus_half = sb("minus_half", [P, WT], scope=scope)

        meta_in = sem("meta_in")
        bias_in = sem("bias_in")
        raw_in = sem("raw_in")
        stage_in = [sem(f"stage_in{s}") for s in range(2)]
        consts = sem("consts")
        consts_zero = sem("consts_zero")
        route_step = sem("route_step")
        sorted_onehot = sem("sorted_onehot")
        sorted_ids = sem("sorted_ids")
        rows_known = sem("rows_known")
        windows_known = sem("windows_known")
        bias_turned = sem("bias_turned")
        bias_ready = sem("bias_ready")
        wT_turned = sem("wT_turned")
        wT_copied = sem("wT_copied")
        folded = sem("folded")
        a_split = sem("a_split")
        chunk_hi = sem("chunk_hi")
        chunk_lo = sem("chunk_lo")
        prepared = sem("prepared")
        x_in = [sem(f"x_in{s}") for s in range(2)]
        xr_split = sem("xr_split")
        xT_turned = sem("xT_turned")
        xT_copied = sem("xT_copied")
        xT_split = sem("xT_split")
        y_done = sem("y_done")
        y_split = sem("y_split")
        scores_done = sem("scores_done")
        softmax_step = sem("softmax_step")
        shifted_ready = sem("shifted_ready")
        exp_ready = sem("exp_ready")
        pd_clear = sem("pd_clear")
        pd_ready = sem("pd_ready")
        z_done = sem("z_done")
        z_split = sem("z_split")
        at_done = sem("at_done")
        at_split = sem("at_split")
        hidden_done = sem("hidden_done")
        gelu_done = sem("gelu_done")
        h_hi_ready = sem("h_hi_ready")
        h_lo_ready = sem("h_lo_ready")
        h_used = sem("h_used")
        cms_copied = sem("cms_copied")
        cms_split = sem("cms_split")
        base_ready = sem("base_ready")
        mod_summed = sem("mod_summed")
        x1_ready = sem("x1_ready")
        aw_free = sem("aw_free")
        aw_in = [sem(f"aw_in{s}") for s in range(2)]
        win_in = sem("win_in")
        win_turned = sem("win_turned")
        xb_ready = sem("xb_ready")
        down_done = sem("down_done")
        hw_ready = sem("hw_ready")
        up_done = sem("up_done")
        norm_step = sem("norm_step")
        var_ready = sem("var_ready")
        rstd_ready = sem("rstd_ready")
        xn_ready = sem("xn_ready")
        xn_turned = sem("xn_turned")
        idx_ready = sem("idx_ready")
        stored = sem("stored")
        window_stored = sem("window_stored")
        half_ready = sem("half_ready")
        waited = sem("waited")

        block = ctx.enter_context(nc.Block())

        def mm3(pe, o, w_hi_ap, w_lo_ap, r_hi_ap, r_lo_ap, first, last):
            pe.matmul(o, w_hi_ap, r_hi_ap, start=first, stop=False)
            pe.matmul(o, w_lo_ap, r_hi_ap, start=False, stop=False)
            return pe.matmul(o, w_hi_ap, r_lo_ap, start=False, stop=last)

        def linked(engine, counter, base):
            n = [0]

            def link(ins):
                n[0] += 1
                ins.then_inc(counter, 1)
                engine.wait_ge(counter, base + n[0])
            return link

        def apart(engine):
            engine.sem_inc(waited, 1)

        PRIMED = 1
        SOFTMAX_STEPS, NORM_STEPS = 6, 4

        @block.sync
        def _(sp):
            sp.dma_start(roles_i[:, :], roles.partition_broadcast(P)).then_inc(meta_in, 16)
            sp.dma_start(role_col_i[:, :], roles.rearrange("(b a) -> b a", a=1)).then_inc(meta_in, 16)
            sp.dma_start(code_col_i[:, :], codes.rearrange("(b a) -> b a", a=1)).then_inc(meta_in, 16)
            for n, w in enumerate((Wq, Wk, Wv, Wp)):
                sp.dma_start(raw[:, n, :, :], w.rearrange("(k p) m -> p k m", p=P)).then_inc(raw_in, 16)
            for at, n, b in ((CB1, 8, cb1), (MB1, 8, mb1), (BP, 2, bp), (CB2, 2, cb2), (MB2, 2, mb2)):
                sp.dma_start(bias_rows[at:at + n, :], b.rearrange("(j p) -> j p", p=P)).then_inc(bias_in, 16)
            n = 0
            for w, k in ((cW1, 1), (cW2, 4), (mW1, 1), (mW2, 4)):
                rows = w.rearrange("(c k p) m -> c p k m", k=k, p=P)
                for c in range(rows.shape[0]):
                    if n >= 2:
                        sp.wait_ge(chunk_lo, n - 1)
                    sp.dma_start(stage[:, n % 2, :].rearrange("p (k m) -> p k m", k=k), rows[c]).then_inc(stage_in[n % 2], 16)
                    n += 1
            assert n == NCHUNK

            sp.wait_ge(windows_known, 1)
            sp.wait_ge(x1_ready, PRIMED + VB * NG)
            sp.sem_inc(aw_free, 2)
            with sp.Fori(0, NW // 2) as pair:
                for s in range(2):
                    j = pair * 2 + s
                    role = sp.value_load(window_meta[0:1, 0, bass.ds(j, 1)], min_val=0, max_val=ROLES - 1)
                    sp.wait_ge(aw_free, j + 1)
                    for layer, (wd, bd, wu, bu, gamma, beta) in enumerate(adapters):
                        sp.dma_start(aw[:, s, layer, 0:V].rearrange("p (k m) -> p k m", k=VB),
                                     wd.rearrange("r (k p) m -> p (r k) m", p=P)[:, bass.ds(role * VB, VB), :])\
                            .then_inc(aw_in[s], 16)
                        sp.dma_start(aw[:, s, layer, V:2 * V],
                                     wu.rearrange("r p m -> p r m")[:, bass.ds(role, 1), :]).then_inc(aw_in[s], 16)
                        sp.dma_start(abd[:, s, layer:layer + 1],
                                     bd.rearrange("r p -> p r")[:, bass.ds(role, 1)]).then_inc(aw_in[s], 16)
                        for n, row in enumerate((bu, gamma, beta)):
                            sp.dma_start(ap_[:, s, layer, n, :],
                                         row[bass.ds(role, 1), :].to_broadcast([P, V])).then_inc(aw_in[s], 16)

        @block.gpsimd
        def _(pool):
            for counter in (window_stored,):
                pool.sem_inc(counter, PRIMED)
            pool.memset(ident[:, :], 0.0).then_inc(consts_zero, 1)
            pool.memset(ones[:, :], 1.0).then_inc(consts, 1)
            pool.iota(batch_id[:, :], [[1, B]], base=0, channel_multiplier=0,
                      allow_small_or_imprecise_dtypes=True).then_inc(consts, 1)
            pool.iota(feature_id[:, :], [[P, VB]], base=0, channel_multiplier=1,
                      allow_small_or_imprecise_dtypes=True).then_inc(consts, 1)
            pool.iota(window_id[:, :], [[1, NW]], base=0, channel_multiplier=0,
                      allow_small_or_imprecise_dtypes=True).then_inc(consts, 1)
            pool.iota(window_start8[:, :], [[WIN, WIN]], base=0, channel_multiplier=0,
                      allow_small_or_imprecise_dtypes=True).then_inc(consts, 1)
            for q in range(Q):
                rows = slice(q * T, (q + 1) * T)
                pool.wait_ge(consts, 5 + 2 * q)
                pool.iota(row_in_batch[rows, :], [[1, 1]], base=0, channel_multiplier=1,
                          allow_small_or_imprecise_dtypes=True).then_inc(consts, 1)
                pool.wait_ge(consts, 6 + 2 * q)
                pool.iota(slot_off[rows, :], [[Q, WT]], base=q, channel_multiplier=0,
                          allow_small_or_imprecise_dtypes=True).then_inc(consts, 1)
            pool.wait_ge(consts_zero, 1)
            pool.wait_ge(consts, CONSTS - 1)
            pool.affine_select(out=ident[:, :], in_=ident[:, :], compare_op=ALU.not_equal, fill=1.0, base=0,
                               pattern=[[-1, P]], channel_multiplier=1).then_inc(consts, 1)
            pool.wait_ge(rows_known, Q)
            for t in range(NG * GT):
                g = t // GT
                if t % GT == 0:
                    pool.wait_ge(prepared, 3)
                if t % GT == 0 and g >= 2:
                    pool.wait_ge(xr_split, 2 * (g - 1))
                    pool.wait_ge(xT_turned, g - 1)
                pool.indirect_dma_start(out=xr[:, g % 2, t % GT, :], out_offset=None, in_=x_rows,
                                        in_offset=bass.IndirectOffsetOnAxis(ap=row_idx[:, t:t + 1], axis=0))\
                    .then_inc(x_in[g % 2], 16)
            pool.wait_ge(x1_ready, PRIMED + VB * NG)
            pool.memset(minus_half[:, :], -0.5).then_inc(half_ready, 1)
            pool.wait_ge(half_ready, 1)
            with pool.Fori(0, NW) as j:
                pool.wait_ge(window_stored, PRIMED + j)
                apart(pool)
                pool.tensor_copy(idx_now[:, :], out_idx[:, bass.ds(j, 1), :].rearrange("p a t -> p (a t)"))\
                    .then_inc(idx_ready, 1)
                for layer in range(LAYERS):
                    pool.wait_ge(var_ready, LAYERS * j + layer + 1)
                    pool.tensor_tensor(rstd[:, :], var_eps[:, :], minus_half[:, :], ALU.pow).then_inc(rstd_ready, 1)
                pool.wait_ge(idx_ready, j + 1)
                pool.wait_ge(xn_ready, LAYERS * (j + 1))
                apart(pool)
                for t in range(WT):
                    pool.indirect_dma_start(out=out_rows, out_offset=bass.IndirectOffsetOnAxis(
                        ap=idx_now[:, t:t + 1], axis=0), in_=xn[:, t, :], in_offset=None,
                        bounds_check=B * T - 1, oob_is_err=False).then_inc(stored, 16)
                pool.wait_ge(stored, 16 * WT * (j + 1))
                pool.sem_inc(window_stored, 1)
            pool.wait_ge(stored, 16 * WT * NW)

        @block.scalar
        def _(act):
            for counter in (gelu_done, at_split):
                act.sem_inc(counter, PRIMED)
            for n in range(3):
                act.wait_ge(wT_turned, n + 1)
                act.activation(wT[:, n, :, :], bank[n][:, :].rearrange("p (k m) -> p k m", k=VB), ACT.Copy)\
                    .then_inc(wT_copied, 1)
            act.wait_ge(bias_turned, 1)
            act.activation(bias[:, :], bank[6][:, 0:22], ACT.Copy).then_inc(bias_ready, 1)
            for n in range(2):
                act.wait_ge(folded, n + 1)
                act.activation(a_hi[:, n, :, :], bank[4 + n][:, :].rearrange("p (k m) -> p k m", k=VB), ACT.Copy)\
                    .then_inc(a_split, 1)
            with act.Fori(0, NCHUNK // 2) as pair:
                for s in range(2):
                    c = pair * 2 + s
                    act.wait_ge(stage_in[s], 16 * (pair + 1))
                    apart(act)
                    act.activation(w_hi[:, bass.ts(c, CHUNK)], stage[:, s, :], ACT.Copy).then_inc(chunk_hi, 1)

            act.wait_ge(bias_ready, 1)
            with act.Fori(0, NG // 2) as pair:
                for s in range(2):
                    g = pair * 2 + s
                    act.wait_ge(x_in[s], 16 * GT * (pair + 1))
                    act.wait_ge(z_done, PRIMED + g)
                    act.activation(xr_hi[:, :, :], xr[:, s, :, :], ACT.Copy).then_inc(xr_split, 1)
                    act.wait_ge(xT_turned, g + 1)
                    apart(act)
                    for vb in range(VB):
                        act.activation(xT[:, vb, bass.ts(g, GR)], bank[vb][:, :], ACT.Copy).then_inc(xT_copied, 1)
                    for vb in range(VB):
                        act.wait_ge(xT_copied, VB * g + vb + 1)
                        apart(act)
                        act.activation(xg_hi[:, vb, :], xT[:, vb, bass.ts(g, GR)], ACT.Copy).then_inc(xT_split, 1)
                    act.wait_ge(y_done, g + 1)
                    for vb in range(VB):
                        act.activation(yz_hi[:, vb, :], bank[2 + vb][:, :], ACT.Copy).then_inc(y_split, 1)
                    act.wait_ge(shifted_ready, g + 1)
                    act.activation(expd[:, :, :], shifted[:, :, :], ACT.Exp, scale=float(V) ** -0.5)\
                        .then_inc(exp_ready, 1)
                    act.wait_ge(z_done, PRIMED + g + 1)
                    for vb in range(VB):
                        act.activation(yz_hi[:, vb, :], bank[5 + vb][:, :], ACT.Copy).then_inc(z_split, 1)
                    act.wait_ge(at_done, g + 1)
                    apart(act)
                    for vb in range(VB):
                        act.activation(at_hi[:, vb, bass.ts(g, GR)], bank[vb][:, :], ACT.Identity,
                                       bias=bias[:, BP + vb:BP + vb + 1]).then_inc(at_split, 1)

            with act.Fori(0, NG) as g:
                for n in range(2 * HB):
                    j = n % HB
                    b = (CB1 if n < HB else MB1) + j
                    act.wait_ge(hidden_done, 2 * HB * g + n + 1)
                    if n < 2:
                        act.wait_ge(h_lo_ready, PRIMED + 2 * HB * g)
                    else:
                        act.wait_ge(h_lo_ready, PRIMED + 2 * HB * g + n - 1)
                    act.activation(h_full[:, n % 2, :], bank[n % 2][:, :], ACT.Gelu, bias=bias[:, b:b + 1])\
                        .then_inc(gelu_done, 1)
                    act.wait_ge(gelu_done, PRIMED + 2 * HB * g + n + 1)
                    if n < 4:
                        act.wait_ge(h_used, PRIMED + 2 * HB * g)
                    else:
                        act.wait_ge(h_used, PRIMED + 2 * HB * g + n - 3)
                    act.activation(h_hi[:, n % 4, :], h_full[:, n % 2, :], ACT.Copy).then_inc(h_hi_ready, 1)
                    if n == HB + 0 - 1:
                        for vb in range(VB):
                            act.wait_ge(cms_copied, VB * g + vb + 1)
                            act.activation(cms_hi[:, vb, :], cms[:, vb, :], ACT.Copy).then_inc(cms_split, 1)

            with act.Fori(0, NW // 2) as pair:
                for s in range(2):
                    j = pair * 2 + s
                    first = act.value_load(window_meta[0:1, 1, bass.ds(j, 1)], min_val=0, max_val=B - WIN)
                    act.wait_ge(x1_ready, PRIMED + VB * NG)
                    act.wait_ge(down_done, PRIMED + LAYERS * j)
                    apart(act)
                    act.activation(xw[:, :, :], xT[:, :, bass.ds(first * T, WR)], ACT.Copy).then_inc(win_in, 1)
                    act.wait_ge(aw_in[s], 288 * (pair + 1))
                    for layer in range(LAYERS):
                        act.wait_ge(down_done, PRIMED + LAYERS * j + layer + 1)
                        act.activation(hw[:, :], bank[0][:, 0:WR], ACT.Gelu,
                                       bias=abd[:, s, layer:layer + 1]).then_inc(hw_ready, 1)
                        if layer < LAYERS - 1:
                            act.wait_ge(xn_turned, (LAYERS - 1) * j + layer + 1)
                            act.activation(xw[:, :, :], bank[3][:, :].rearrange("p (k m) -> p k m", k=VB), ACT.Copy)\
                                .then_inc(win_in, 1)

        @block.vector
        def _(dve):
            for counter in (h_lo_ready, x1_ready, xb_ready):
                dve.sem_inc(counter, PRIMED)
            link = linked(dve, route_step, 0)
            dve.wait_ge(meta_in, 48)
            dve.wait_ge(consts, CONSTS)
            role_row, key_row, onehot, scratch = (rt[:, n, :] for n in range(4))
            role_c, code_c, key_c, rank_c, neg_c = (rc[:, n:n + 1] for n in range(5))
            link(dve.tensor_copy(code_c, code_col_i[:, :]))
            link(dve.tensor_copy(role_row, roles_i[:, :]))
            link(dve.tensor_copy(role_c, role_col_i[:, :]))
            for r, neg in ((role_row, scratch), (role_c, neg_c)):
                link(dve.tensor_scalar(neg, r, 0.0, float(ROLES), ALU.is_lt, ALU.mult))
                link(dve.tensor_tensor(r, r, neg, ALU.add))
                link(dve.tensor_scalar(r, r, 0.0, float(ROLES - 1), ALU.max, ALU.min))
            link(dve.scalar_tensor_tensor(key_row, role_row, float(B), batch_id[:, :], ALU.mult, ALU.add))
            link(dve.scalar_tensor_tensor(key_c, role_c, float(B), feature_id[0:B, 0:1], ALU.mult, ALU.add))
            link(dve.tensor_scalar(scratch[0:B, :], key_row[0:B, :], key_c, None, ALU.is_lt))
            link(dve.tensor_reduce(rank_c, scratch[0:B, :], AX.X, ALU.add))
            link(dve.tensor_scalar(onehot[0:B, :], batch_id[0:B, :], rank_c, None, ALU.is_equal))
            link(dve.tensor_scalar(pick[0:B, 0:2, :].rearrange("p a b -> p (a b)"), ones[:, :],
                                   feature_id[0:B, 0:1], None, ALU.mult))
            dve.tensor_scalar(pick[0:B, 2:4, :].rearrange("p a b -> p (a b)"), ones[:, :],
                              code_c, None, ALU.mult).then_inc(sorted_onehot, 1)
            dve.wait_ge(sorted_ids, 1)
            dve.wait_ge(bias_ready, 1)
            sorted_batch, sorted_code = bank[7][:, 0:B], bank[7][:, B:2 * B]
            for q in range(Q):
                rows = slice(q * T, (q + 1) * T)
                dve.tensor_scalar(row_idx[rows, :], bank[7][rows, q:B:Q], float(T), row_in_batch[rows, :],
                                  ALU.mult, ALU.add).then_inc(rows_known, 1)
            for vb in range(VB):
                link(dve.tensor_scalar(cms_bias[:, vb, :], sorted_code, feature_id[:, vb:vb + 1],
                                       bias[:, CB2 + vb:CB2 + vb + 1], ALU.is_equal, ALU.add))
            place_row = key_row
            link(dve.tensor_scalar(place_row, sorted_batch, float(T), row_in_batch[:, :], ALU.mult, ALU.add))
            n0, n1, n2, o2, w1, w2, u1, u2 = (rs[:, n:n + 1] for n in range(8))
            for r, n in ((0, n0), (1, n1)):
                link(dve.tensor_scalar(scratch, role_row, float(r), None, ALU.is_equal))
                link(dve.tensor_reduce(n, scratch, AX.X, ALU.add))
            link(dve.tensor_tensor(o2, n0, n1, ALU.add))
            link(dve.tensor_scalar(n2, o2, -1.0, float(B), ALU.mult, ALU.add))
            for n, w in ((n0, w1), (n1, w2)):
                link(dve.tensor_scalar(scratch[:, 0:WIN], window_start8[:, :], n, None, ALU.is_lt))
                link(dve.tensor_reduce(w, scratch[:, 0:WIN], AX.X, ALU.add))
            link(dve.tensor_tensor(w2, w2, w1, ALU.add))
            link(dve.scalar_tensor_tensor(u1, w1, -float(WIN), n0, ALU.mult, ALU.add))
            link(dve.scalar_tensor_tensor(u2, w2, -float(WIN), o2, ALU.mult, ALU.add))
            link(dve.tensor_tensor(u2, u2, u1, ALU.subtract))
            in1, in2, start, end, first, role_w = (rw[:, n, 0:NW] for n in range(6))
            slot, ok, found, hit = (rw[:, n, :].rearrange("p (j t) -> p j t", t=WT) for n in range(6, 10))
            link(dve.tensor_scalar(in1, window_id[:, :], w1, None, ALU.is_ge))
            link(dve.tensor_scalar(in2, window_id[:, :], w2, None, ALU.is_ge))
            link(dve.tensor_tensor(role_w, in1, in2, ALU.add))
            link(dve.tensor_scalar(start, window_id[:, :], float(WIN), None, ALU.mult))
            link(dve.scalar_tensor_tensor(start, in1, u1, start, ALU.mult, ALU.add))
            link(dve.scalar_tensor_tensor(start, in2, u2, start, ALU.mult, ALU.add))
            link(dve.tensor_scalar(end, in1, n1, n0, ALU.mult, ALU.add))
            link(dve.scalar_tensor_tensor(end, in2, n2, end, ALU.mult, ALU.add))
            link(dve.tensor_scalar(first, start, float(B - WIN), None, ALU.min))
            link(dve.tensor_copy(window_meta[:, 0, :], role_w))
            link(dve.tensor_copy(window_meta[:, 1, :], first))
            wide = [P, NW, WT]
            link(dve.tensor_tensor(slot, first.unsqueeze(2).to_broadcast(wide),
                                   slot_off[:, :].unsqueeze(1).to_broadcast(wide), ALU.add))
            link(dve.tensor_tensor(ok, slot, start.unsqueeze(2).to_broadcast(wide), ALU.is_ge))
            link(dve.tensor_tensor(hit, slot, end.unsqueeze(2).to_broadcast(wide), ALU.is_lt))
            link(dve.tensor_tensor(ok, ok, hit, ALU.mult))
            flat = [P, NW * WT, B]
            link(dve.tensor_tensor(pick[:, :, :], rw[:, 6, :].unsqueeze(2).to_broadcast(flat),
                                   batch_id[:, :].unsqueeze(1).to_broadcast(flat), ALU.is_equal))
            link(dve.tensor_tensor(pick[:, :, :], pick[:, :, :], place_row.unsqueeze(1).to_broadcast(flat), ALU.mult))
            link(dve.tensor_reduce(rw[:, 8, :], pick[:, :, :], AX.X, ALU.add))
            link(dve.scalar_tensor_tensor(found, ok, -float(OUT_OF_RANGE), found, ALU.mult, ALU.add))
            dve.tensor_scalar(out_idx[:, :, :], found, float(OUT_OF_RANGE), None, ALU.add).then_inc(windows_known, 1)

            for n in range(2):
                dve.wait_ge(a_split, n + 1)
                dve.tensor_tensor(a_lo[:, n, :, :], bank[4 + n][:, :].rearrange("p (k m) -> p k m", k=VB),
                                  a_hi[:, n, :, :].bitcast(F32), ALU.subtract).then_inc(prepared, 1)
            with dve.Fori(0, NCHUNK // 2) as pair:
                for s in range(2):
                    c = pair * 2 + s
                    dve.wait_ge(chunk_hi, c + 1)
                    dve.tensor_tensor(w_lo[:, bass.ts(c, CHUNK)], stage[:, s, :],
                                      w_hi[:, bass.ts(c, CHUNK)].bitcast(F32), ALU.subtract).then_inc(chunk_lo, 1)
            dve.wait_ge(chunk_lo, NCHUNK)
            dve.memset(pd_hi[:, :, :].bitcast(F32), 0.0).then_inc(pd_clear, 1)
            dve.memset(pd_lo[:, :, :].bitcast(F32), 0.0).then_inc(prepared, 1)
            dve.wait_ge(pd_clear, 1)

            with dve.Fori(0, NG // 2) as pair:
                for s in range(2):
                    g = pair * 2 + s
                    dve.wait_ge(xr_split, 2 * g + 1)
                    dve.tensor_tensor(xr_lo[:, :, :], xr[:, s, :, :], xr_hi[:, :, :].bitcast(F32), ALU.subtract)\
                        .then_inc(xr_split, 1)
                    for vb in range(VB):
                        dve.wait_ge(xT_split, 2 * VB * g + VB)
                        dve.tensor_tensor(xg_lo[:, vb, :], xT[:, vb, bass.ts(g, GR)],
                                          xg_hi[:, vb, :].bitcast(F32), ALU.subtract).then_inc(xT_split, 1)
                    for vb in range(VB):
                        dve.wait_ge(y_split, 2 * VB * g + VB)
                        dve.tensor_tensor(yz_lo[:, vb, :], bank[2 + vb][:, :], yz_hi[:, vb, :].bitcast(F32),
                                          ALU.subtract).then_inc(y_split, 1)
                    link = linked(dve, softmax_step, SOFTMAX_STEPS * g)
                    dve.wait_ge(scores_done, g + 1)
                    own = [bank[4][q * T:(q + 1) * T, :].rearrange("p (i c) -> p i c", c=P)[:, :, q * T:(q + 1) * T]
                           for q in range(Q)]
                    for q in range(Q):
                        ins = dve.tensor_reduce(row_max[q * T:(q + 1) * T, :], own[q], AX.X, ALU.max)
                    link(ins)
                    for q in range(Q):
                        ins = dve.tensor_tensor(shifted[q * T:(q + 1) * T, :, :], own[q],
                                                row_max[q * T:(q + 1) * T, :].unsqueeze(2).to_broadcast([T, GT, T]),
                                                ALU.subtract)
                    ins.then_inc(shifted_ready, 1)
                    dve.wait_ge(exp_ready, g + 1)
                    link(dve.tensor_reduce(row_sum[:, 0, :], expd[:, :, :], AX.X, ALU.add))
                    link(dve.reciprocal(row_sum[:, 1, :], row_sum[:, 0, :]))
                    link(dve.tensor_tensor(prob[:, :, :], expd[:, :, :],
                                           row_sum[:, 1, :].unsqueeze(2).to_broadcast([P, GT, T]), ALU.mult))
                    link(dve.transpose(probT[:, :, :], prob[:, :, :]))
                    for q in range(Q):
                        rows = slice(q * T, (q + 1) * T)
                        ins = dve.tensor_copy(pd_hi[rows, :, rows], probT[rows, :, :])
                    link(ins)
                    for q in range(Q):
                        rows = slice(q * T, (q + 1) * T)
                        ins = dve.tensor_tensor(pd_lo[rows, :, rows], probT[rows, :, :],
                                                pd_hi[rows, :, rows].bitcast(F32), ALU.subtract)
                    ins.then_inc(pd_ready, 1)
                    for vb in range(VB):
                        dve.wait_ge(z_split, 2 * VB * g + VB)
                        dve.tensor_tensor(yz_lo[:, vb, :], bank[5 + vb][:, :], yz_hi[:, vb, :].bitcast(F32),
                                          ALU.subtract).then_inc(z_split, 1)
                    for vb in range(VB):
                        dve.wait_ge(at_split, PRIMED + 2 * VB * g + VB)
                        dve.scalar_tensor_tensor(at_lo[:, vb, bass.ts(g, GR)], bank[vb][:, :],
                                                 bias[:, BP + vb:BP + vb + 1],
                                                 at_hi[:, vb, bass.ts(g, GR)].bitcast(F32), ALU.add, ALU.subtract)\
                            .then_inc(at_split, 1)

            with dve.Fori(0, NG) as g:
                for n in range(2 * HB):
                    dve.wait_ge(h_hi_ready, 2 * HB * g + n + 1)
                    dve.tensor_tensor(h_lo[:, n % 4, :], h_full[:, n % 2, :], h_hi[:, n % 4, :].bitcast(F32),
                                      ALU.subtract).then_inc(h_lo_ready, 1)
                    if n == HB - 1:
                        dve.wait_ge(h_used, PRIMED + 2 * HB * g + HB)
                        dve.wait_ge(x1_ready, PRIMED + VB * g)
                        for vb in range(VB):
                            dve.tensor_tensor(
                                cms[:, vb, :].rearrange("p (b t) -> p b t", t=T),
                                bank[2 + vb][:, :].rearrange("p (b t) -> p b t", t=T),
                                cms_bias[:, vb, bass.ts(g, GB)].unsqueeze(2).to_broadcast([P, GB, T]), ALU.add)\
                                .then_inc(cms_copied, 1)
                        for vb in range(VB):
                            dve.wait_ge(cms_split, 2 * VB * g + VB)
                            dve.tensor_tensor(cms_lo[:, vb, :], cms[:, vb, :], cms_hi[:, vb, :].bitcast(F32),
                                              ALU.subtract).then_inc(cms_split, 1)
                        for vb in range(VB):
                            dve.tensor_tensor(xT[:, vb, bass.ts(g, GR)], xT[:, vb, bass.ts(g, GR)], cms[:, vb, :],
                                              ALU.add).then_inc(base_ready, 1)
                dve.wait_ge(h_used, PRIMED + 2 * HB * (g + 1))
                dve.wait_ge(base_ready, VB * (g + 1))
                for vb in range(VB):
                    dve.scalar_tensor_tensor(cms[:, vb, :], bank[4 + vb][:, :], bias[:, MB2 + vb:MB2 + vb + 1],
                                             xT[:, vb, bass.ts(g, GR)], ALU.add, ALU.add).then_inc(mod_summed, 1)
                for vb in range(VB):
                    dve.wait_ge(mod_summed, VB * g + vb + 1)
                    dve.tensor_scalar(xT[:, vb, bass.ts(g, GR)], cms[:, vb, :], 0.0, 1.0, ALU.max, ALU.min)\
                        .then_inc(x1_ready, 1)

            with dve.Fori(0, NW // 2) as pair:
                for s in range(2):
                    j = pair * 2 + s
                    dve.wait_ge(aw_in[s], 288 * (pair + 1))
                    rows2 = [P, WT, V]

                    def par(layer, n):
                        return ap_[:, s, layer, n, :].unsqueeze(1).to_broadcast(rows2)
                    link = linked(dve, norm_step, NORM_STEPS * LAYERS * j)
                    dve.wait_ge(win_turned, j + 1)
                    dve.tensor_tensor(xb[:, :, :], bank[1][:, :].rearrange("p (t v) -> p t v", t=WT), par(0, 0),
                                      ALU.add).then_inc(xb_ready, 1)
                    for layer in range(LAYERS):
                        dve.wait_ge(up_done, LAYERS * j + layer + 1)
                        dve.wait_ge(xb_ready, PRIMED + LAYERS * j + layer + 1)
                        link(dve.tensor_tensor(yw[:, :, :], bank[2][:, :].rearrange("p (t v) -> p t v", t=WT),
                                               xb[:, :, :], ALU.add))
                        for t in range(WT):
                            ins = dve.bn_stats(stats[:, t, :], yw[:, t, :])
                        link(ins)
                        apart(dve)
                        for t in range(WT):
                            ins = dve.bn_aggr(moments[:, t, :], stats[:, t, :])
                        link(ins)
                        dve.tensor_scalar(var_eps[:, :], moments[:, :, 1:2].rearrange("p t a -> p (t a)"), EPS, None,
                                          ALU.add).then_inc(var_ready, 1)
                        for t in range(WT):
                            ins = dve.scalar_tensor_tensor(yw[:, t, :], yw[:, t, :], moments[:, t, 0:1],
                                                           ap_[:, s, layer, 1, :], ALU.subtract, ALU.mult)
                        link(ins)
                        dve.wait_ge(rstd_ready, LAYERS * j + layer + 1)
                        if layer == 0:
                            dve.wait_ge(window_stored, PRIMED + j)
                        else:
                            dve.wait_ge(xn_turned, (LAYERS - 1) * j + layer)
                        for t in range(WT):
                            ins = dve.scalar_tensor_tensor(xn[:, t, :], yw[:, t, :], rstd[:, t:t + 1],
                                                           ap_[:, s, layer, 2, :], ALU.mult, ALU.add)
                        ins.then_inc(xn_ready, 1)
                        dve.wait_ge(xn_ready, LAYERS * j + layer + 1)
                        if layer < LAYERS - 1:
                            dve.tensor_tensor(xb[:, :, :], xn[:, :, :], par(layer + 1, 0), ALU.add)\
                                .then_inc(xb_ready, 1)
                        else:
                            dve.sem_inc(aw_free, 1)

        @block.tensor
        def _(pe):
            for counter in (z_done, h_used, down_done):
                pe.sem_inc(counter, PRIMED)
            pe.wait_ge(consts, CONSTS)
            for n in range(3):
                pe.wait_ge(raw_in, 16 * 4)
                for eb in range(VB):
                    for db in range(VB):
                        ins = pe.transpose(bank[n][:, eb * V + db * P:eb * V + (db + 1) * P],
                                           raw[:, n, db, eb * P:(eb + 1) * P], ident[:, :])
                ins.then_inc(wT_turned, 1)
            pe.wait_ge(bias_in, 16 * 5)
            pe.transpose(bank[6][:, 0:22], bias_rows[:, :], ident[0:22, 0:22]).then_inc(bias_turned, 1)
            for n, (lhs, rhs) in enumerate(((wT[:, 0], wT[:, 1]), (wT[:, 2], raw[:, 3]))):
                pe.wait_ge(wT_copied, 2 + n)
                for db in range(VB):
                    for eb in range(VB):
                        ins = pe.matmul(bank[4 + n][:, db * V:(db + 1) * V], lhs[:, eb, db * P:(db + 1) * P],
                                        rhs[:, eb, :], start=(eb == 0), stop=(eb == VB - 1))
                ins.then_inc(folded, 1)
            pe.wait_ge(sorted_onehot, 1)
            for n in range(2):
                ins = pe.matmul(bank[7][:, n * B:(n + 1) * B], pick[0:B, 2 * n:2 * n + 2, :].rearrange("p a b -> p (a b)"),
                                rt[0:B, 2, :], start=True, stop=True)
            ins.then_inc(sorted_ids, 1)

            pe.wait_ge(prepared, 3)
            with pe.Fori(0, NG // 2) as pair:
                for s in range(2):
                    g = pair * 2 + s
                    pe.wait_ge(x_in[s], 16 * GT * (pair + 1))
                    pe.wait_ge(at_split, PRIMED + 2 * VB * g)
                    for vb in range(VB):
                        for i in range(GT):
                            ins = pe.transpose(bank[vb][:, i * P:(i + 1) * P], xr[:, s, i, vb * P:(vb + 1) * P],
                                               ident[:, :])
                    ins.then_inc(xT_turned, 1)
                    pe.wait_ge(xT_split, 2 * VB * (g + 1))
                    for ob in range(VB):
                        for k in range(VB):
                            cols = slice(ob * P, (ob + 1) * P)
                            ins = mm3(pe, bank[2 + ob][:, :], a_hi[:, 0, k, cols], a_lo[:, 0, k, cols],
                                      xg_hi[:, k, :], xg_lo[:, k, :], k == 0, k == VB - 1)
                    ins.then_inc(y_done, 1)
                    pe.wait_ge(y_split, 2 * VB * (g + 1))
                    for i in range(GT):
                        cols = slice(i * P, (i + 1) * P)
                        for k in range(VB):
                            ins = mm3(pe, bank[4][:, cols], yz_hi[:, k, cols], yz_lo[:, k, cols],
                                      xg_hi[:, k, cols], xg_lo[:, k, cols], k == 0, k == VB - 1)
                    ins.then_inc(scores_done, 1)
                    pe.wait_ge(xr_split, 2 * (g + 1))
                    pe.wait_ge(pd_ready, g + 1)
                    for vb in range(VB):
                        for i in range(GT):
                            ins = mm3(pe, bank[5 + vb][:, i * P:(i + 1) * P], xr_hi[:, i, vb * P:(vb + 1) * P],
                                      xr_lo[:, i, vb * P:(vb + 1) * P], pd_hi[:, i, :], pd_lo[:, i, :], True, True)
                    ins.then_inc(z_done, 1)
                    pe.wait_ge(z_split, 2 * VB * (g + 1))
                    for ob in range(VB):
                        for k in range(VB):
                            cols = slice(ob * P, (ob + 1) * P)
                            ins = mm3(pe, bank[ob][:, :], a_hi[:, 1, k, cols], a_lo[:, 1, k, cols],
                                      yz_hi[:, k, :], yz_lo[:, k, :], k == 0, k == VB - 1)
                    ins.then_inc(at_done, 1)

            pe.wait_ge(chunk_lo, NCHUNK)
            pe.wait_ge(at_split, PRIMED + 2 * VB * NG)
            with pe.Fori(0, NG) as g:
                def hidden(n, parts):
                    w, j = (CW1, n) if n < HB else (MW1, n - HB)
                    k_all = VB if n < HB else 2 * VB
                    if 0 in parts:
                        if n < 2:
                            pe.wait_ge(gelu_done, PRIMED + 2 * HB * g)
                        else:
                            pe.wait_ge(gelu_done, PRIMED + 2 * HB * g + n - 1)
                    if 1 in parts and n >= HB:
                        pe.wait_ge(cms_split, 2 * VB * (g + 1))
                    ins = None
                    for k in range(k_all):
                        if k // VB not in parts:
                            continue
                        cols = slice(w + k * H + j * P, w + k * H + (j + 1) * P)
                        r_hi, r_lo = ((at_hi[:, k, bass.ts(g, GR)], at_lo[:, k, bass.ts(g, GR)]) if k < VB
                                      else (cms_hi[:, k - VB, :], cms_lo[:, k - VB, :]))
                        ins = mm3(pe, bank[n % 2][:, :], w_hi[:, cols], w_lo[:, cols], r_hi, r_lo,
                                  k == 0, k == k_all - 1)
                    if n < HB or 1 in parts:
                        ins.then_inc(hidden_done, 1)

                def project(n):
                    w, j, acc = (CW2, n, 2) if n < HB else (MW2, n - HB, 4)
                    pe.wait_ge(h_hi_ready, 2 * HB * g + n + 1)
                    for ob in range(VB):
                        cols = slice(w + j * V + ob * P, w + j * V + (ob + 1) * P)
                        pe.matmul(bank[acc + ob][:, :], w_hi[:, cols], h_hi[:, n % 4, :], start=(j == 0), stop=False)
                        pe.matmul(bank[acc + ob][:, :], w_lo[:, cols], h_hi[:, n % 4, :], start=False, stop=False)
                    pe.wait_ge(h_lo_ready, PRIMED + 2 * HB * g + n + 1)
                    for ob in range(VB):
                        cols = slice(w + j * V + ob * P, w + j * V + (ob + 1) * P)
                        ins = pe.matmul(bank[acc + ob][:, :], w_hi[:, cols], h_lo[:, n % 4, :], start=False,
                                        stop=(j == HB - 1))
                        if ob == VB - 1:
                            ins.then_inc(h_used, 1)
                    return ins

                hidden(0, (0, 1))
                hidden(1, (0, 1))
                for n in range(HB - 2):
                    project(n)
                    hidden(n + 2, (0, 1))
                project(HB - 2)
                hidden(HB, (0,))
                project(HB - 1)
                hidden(HB + 1, (0,))
                hidden(HB, (1,))
                hidden(HB + 1, (1,))
                for n in range(HB, 2 * HB - 2):
                    project(n)
                    hidden(n + 2, (0, 1))
                project(2 * HB - 2)
                project(2 * HB - 1)

            with pe.Fori(0, NW // 2) as pair:
                for s in range(2):
                    j = pair * 2 + s
                    pe.wait_ge(aw_in[s], 288 * (pair + 1))
                    for layer in range(LAYERS):
                        pe.wait_ge(win_in, LAYERS * j + layer + 1)
                        if layer == 0:
                            pe.wait_ge(xb_ready, PRIMED + LAYERS * j)
                            for t in range(WT):
                                for vb in range(VB):
                                    ins = pe.transpose(bank[1][:, t * V + vb * P:t * V + (vb + 1) * P],
                                                       xw[:, vb, t * P:(t + 1) * P], ident[:, :])
                            ins.then_inc(win_turned, 1)
                        for vb in range(VB):
                            ins = pe.matmul(bank[0][:, 0:WR], aw[:, s, layer, vb * KD:(vb + 1) * KD], xw[:, vb, :],
                                            start=(vb == 0), stop=(vb == VB - 1))
                        ins.then_inc(down_done, 1)
                        pe.wait_ge(hw_ready, LAYERS * j + layer + 1)
                        for t in range(WT):
                            ins = pe.matmul(bank[2][:, t * V:(t + 1) * V], hw[:, t * P:(t + 1) * P],
                                            aw[:, s, layer, V:2 * V], start=True, stop=True)
                        ins.then_inc(up_done, 1)
                        pe.wait_ge(xn_ready, LAYERS * j + layer + 1)
                        if layer < LAYERS - 1:
                            for vb in range(VB):
                                for t in range(WT):
                                    ins = pe.transpose(bank[3][:, vb * WR + t * P:vb * WR + (t + 1) * P],
                                                       xn[:, t, vb * P:(vb + 1) * P], ident[:, :])
                            ins.then_inc(xn_turned, 1)


_ADAPTER = [("W_down", "b_down", "W_up", "b_up", "gamma", "beta"),
            ("W_down", "b_down", "W_up", "b_up", "ln_w", "ln_b"),
            ("W_down", "b_down", "W_up", "b_up", "ln_w", "ln_b")]
_INS = ["x", "itok_B_17_1546", "itok_B_1_2"] + ["L0_cond_" + n for n in (
    "Wq", "Wk", "Wv", "Wp", "bp", "cW1", "cb1", "cW2", "cb2", "mW1", "mb1", "mW2", "mb2")]
_INS_ADAPTERS = [[f"L{i + 1}_cond_{n}" for n in names] for i, names in enumerate(_ADAPTER)]


def kernel(**inputs):
    import numpy as _np
    import concourse.bacc as _bacc
    from concourse import mybir as _mybir
    from concourse.bass_utils import run_bass_kernel_spmd as _run

    nc = _bacc.Bacc("TRN2", target_bir_lowering=False, num_devices=1)
    arrays = {}

    def declare(name):
        a = _np.ascontiguousarray(inputs[name])
        arrays[f"in_{name}"] = a
        return nc.dram_tensor(f"in_{name}", a.shape, _mybir.dt.from_np(a.dtype), kind="ExternalInput").ap()

    args = [declare(n) for n in _INS]
    adapters = [[declare(n) for n in names] for names in _INS_ADAPTERS]
    out = nc.dram_tensor("out_0", (64, 32, 256), _mybir.dt.float32, kind="ExternalOutput").ap()
    build(nc, *args, adapters, out)
    r = _run(nc, [arrays], core_ids=[0])
    return r.results[0]["out_0"]
```

```python
from contextlib import ExitStack

import concourse.bass as bass
from concourse import mybir

F32 = mybir.dt.float32
F32R = mybir.dt.float32r
I32 = mybir.dt.int32
ALU = mybir.AluOpType
ACT = mybir.ActivationFunctionType
AX = mybir.AxisListType

P = 128
B, T, V = 64, 32, 256
H = 4 * V
KD = 128
ROLES, LAYERS = 3, 3
VB = V // P
HB = H // P
Q = P // T
GT = 4
GR = GT * P
GB = GT * Q
NG = B // GB
WIN = 8
WR = WIN * T
WT = WR // P
NW = B // WIN + ROLES - 1
EPS = 1e-5
OUT_OF_RANGE = 4096

CW1, CW2, MW1, MW2 = 0, 2 * H, 4 * H, 8 * H
CHUNK = 1024
NCHUNK = 10
STAGES = 6


def build(nc, x, codes, roles, Wq, Wk, Wv, Wp, bp, cW1, cb1, cW2, cb2, mW1, mb1, mW2, mb2, adapters, out):
    x_rows = x.rearrange("b t v -> (b t) v")
    out_rows = out.rearrange("b t v -> (b t) v")

    with ExitStack() as ctx:
        def sb(name, shape, dt=F32, scope=ctx):
            return scope.enter_context(nc.sbuf_tensor(name, shape, dt))

        def sem(name):
            return ctx.enter_context(nc.semaphore(name))

        bank = [ctx.enter_context(nc.psum_tensor(f"bank{i}", [P, GR], F32)) for i in range(8)]

        ident = sb("ident", [P, P])
        ones = sb("ones", [B, P])
        batch_id = sb("batch_id", [P, B])
        feature_id = sb("feature_id", [P, VB])
        row_in_batch = sb("row_in_batch", [P, 1])
        window_id = sb("window_id", [P, NW])
        window_start8 = sb("window_start8", [P, WIN])
        slot_off = sb("slot_off", [P, WT])
        roles_i = sb("roles_i", [P, B], I32)
        role_col_i = sb("role_col_i", [B, 1], I32)
        code_col_i = sb("code_col_i", [B, 1], I32)
        row_idx = sb("row_idx", [P, NG * GT], I32)
        out_idx = sb("out_idx", [P, NW, WT], I32)
        window_meta = sb("window_meta", [P, 2, NW], I32)
        cms_bias = sb("cms_bias", [P, VB, B])
        bias_rows = sb("bias_rows", [22, P])
        bias = sb("bias", [P, 22])
        CONSTS = 6 + 2 * Q
        CB1, MB1, BP, CB2, MB2 = 0, 8, 16, 18, 20

        packed_w = nc.dram_tensor("packed_w", (ROLES, LAYERS, P, 2 * V + 1), F32).ap()
        packed_rows = nc.dram_tensor("packed_rows", (ROLES, LAYERS, 3, V), F32).ap()

        fold = sb("fold", [P, 2, VB, V])
        xT = sb("xT", [P, VB, NG * GR])

        xr = sb("xr", [P, GT, V])
        yz = sb("yz", [P, VB, GR])
        pd = sb("pd", [P, GT, P])
        row_max = sb("row_max", [P, GT])
        shifted = sb("shifted", [P, GT, T])
        expd = sb("expd", [P, GT, T])
        row_sum = sb("row_sum", [P, 2, GT])
        prob = sb("prob", [P, GT, T])
        probT = sb("probT", [P, GT, T])
        at_hi = sb("at_hi", [P, VB, GR], F32R)
        at_lo = sb("at_lo", [P, VB, GR], F32R)

        class Slot:
            def __init__(self, n, scope):
                self.w = sb(f"adapter_w{n}", [P, LAYERS, 2 * V + 1], scope=scope)
                self.rows = sb(f"adapter_rows{n}", [P, LAYERS, 3, V], scope=scope)
                self.xT = sb(f"window_xT{n}", [P, VB, WR], scope=scope)
                self.y = sb(f"window_y{n}", [P, WT, V], scope=scope)
                self.h = sb(f"window_h{n}", [P, WR], scope=scope)
                self.x = sb(f"window_x{n}", [P, WT, V], scope=scope)
                self.stats = sb(f"stats{n}", [P, WT, 6], scope=scope)
                self.moments = sb(f"moments{n}", [P, WT, 2], scope=scope)
                self.var = sb(f"var_eps{n}", [P, WT], scope=scope)
                self.rstd = sb(f"rstd{n}", [P, WT], scope=scope)
                self.idx = sb(f"store_idx{n}", [P, WT], I32, scope=scope)
                self.bank = bank[(6, 7, 4, 5)[n]]
                self.loaded = [sem(f"adapter_loaded{n}_{layer}") for layer in range(LAYERS)]
                self.x_in = sem(f"window_x_in{n}")
                self.turned = sem(f"window_turned{n}")
                self.y_ready = sem(f"window_y_ready{n}")
                self.down_done = sem(f"down_done{n}")
                self.h_ready = sem(f"window_h_ready{n}")
                self.up_done = sem(f"up_done{n}")
                self.norm_step = sem(f"norm_step{n}")
                self.var_ready = sem(f"var_ready{n}")
                self.rstd_ready = sem(f"rstd_ready{n}")
                self.x_ready = sem(f"window_x_ready{n}")
                self.layer_done = [sem(f"layer_done{n}_{layer}") for layer in range(LAYERS)]
                self.idx_ready = sem(f"idx_ready{n}")
                self.stored = sem(f"stored{n}")

        packed = sem("packed")
        minus_half = sb("minus_half", [P, WT])

        with ExitStack() as scope:
            stage = sb("stage", [P, STAGES, CHUNK], scope=scope)
            raw = sb("raw", [P, 4, VB, V], scope=scope)
            wT = sb("wT", [P, 3, VB, V], scope=scope)
            rt = sb("rt", [P, 4, B], scope=scope)
            rc = sb("rc", [B, 8], scope=scope)
            rs = sb("rs", [P, 32], scope=scope)
            rw = sb("rw", [P, 10, NW * WT], scope=scope)
            pick = sb("pick", [P, NW * WT, B], scope=scope)
        slots = [Slot(n, ctx) for n in range(2)]
        h_full = sb("h_full", [P, 2, GR])
        h_hi = sb("h_hi", [P, 2, GR], F32R)
        h_lo = sb("h_lo", [P, 2, GR], F32R)
        cms = sb("cms", [P, VB, GR])
        cms_hi = sb("cms_hi", [P, VB, GR], F32R)
        cms_lo = sb("cms_lo", [P, VB, GR], F32R)
        with ExitStack() as scope:
            w_hi = sb("w_hi", [P, NCHUNK * CHUNK], F32R, scope)
            w_lo = sb("w_lo", [P, NCHUNK * CHUNK], F32R, scope)
        slots += [Slot(n, ctx) for n in range(2, 4)]

        meta_in = sem("meta_in")
        bias_in = sem("bias_in")
        raw_in = sem("raw_in")
        consts = sem("consts")
        consts_zero = sem("consts_zero")
        route_step = sem("route_step")
        sorted_onehot = sem("sorted_onehot")
        sorted_ids = sem("sorted_ids")
        rows_known = sem("rows_known")
        windows_known = sem("windows_known")
        bias_turned = sem("bias_turned")
        bias_ready = sem("bias_ready")
        wT_turned = sem("wT_turned")
        wT_copied = sem("wT_copied")
        folded = sem("folded")
        fold_ready = sem("fold_ready")
        chunk_hi = sem("chunk_hi")
        chunk_lo = sem("chunk_lo")
        prepared = sem("prepared")
        x_in = sem("x_in")
        xT_turned = sem("xT_turned")
        xT_ready = sem("xT_ready")
        y_done = sem("y_done")
        y_ready = sem("y_ready")
        scores_done = sem("scores_done")
        softmax_step = sem("softmax_step")
        shifted_ready = sem("shifted_ready")
        exp_ready = sem("exp_ready")
        pd_clear = sem("pd_clear")
        pd_ready = sem("pd_ready")
        z_done = sem("z_done")
        z_ready = sem("z_ready")
        at_done = sem("at_done")
        at_split = sem("at_split")
        hidden_done = sem("hidden_done")
        gelu_done = sem("gelu_done")
        h_hi_ready = sem("h_hi_ready")
        h_lo_ready = sem("h_lo_ready")
        h_used = sem("h_used")
        cms_copied = sem("cms_copied")
        cms_split = sem("cms_split")
        base_ready = sem("base_ready")
        mod_summed = sem("mod_summed")
        x1_ready = sem("x1_ready")
        window_done = sem("window_done")
        half_ready = sem("half_ready")
        waited = sem("waited")
        stage_in = [sem(f"stage_in{s}") for s in range(STAGES)]

        block = ctx.enter_context(nc.Block())

        def mm3(pe, o, w_hi_ap, w_lo_ap, r_hi_ap, r_lo_ap, first, last):
            pe.matmul(o, w_hi_ap, r_hi_ap, start=first, stop=False)
            pe.matmul(o, w_lo_ap, r_hi_ap, start=False, stop=False)
            return pe.matmul(o, w_hi_ap, r_lo_ap, start=False, stop=last)

        def linked(engine, counter, base):
            n = [0]

            def link(ins):
                n[0] += 1
                ins.then_inc(counter, 1)
                engine.wait_ge(counter, base + n[0])
            return link

        def apart(engine):
            engine.sem_inc(waited, 1)

        def quarter(q):
            return slice(q * T, (q + 1) * T)

        def two(ap):
            return ap.rearrange("p (k m) -> p k m", k=2)

        PRIMED = 1
        SOFTMAX_STEPS, NORM_STEPS = 5, 4

        core = [("H", 0), ("H", 1)]
        for n in range(HB - 2):
            core += [("D", n), ("H", n + 2)]
        core += [("D", HB - 2), ("Ha", HB), ("D", HB - 1), ("C", 0), ("Ha", HB + 1), ("Hb", HB), ("Hb", HB + 1)]
        for n in range(HB, 2 * HB - 2):
            core += [("D", n), ("H", n + 2)]
        core += [("D", 2 * HB - 2), ("D", 2 * HB - 1), ("F", 0)]
        ATTENTION = {("H", 2): ["X"], ("H", 3): ["Y"], ("H", 5): ["S"], ("H", 6): ["P"], ("Hb", HB + 1): ["Z"],
                     ("H", 2 * HB - 1): ["A"]}
        WINDOWS = {("H", 0): [("load", 0, 0), ("load", 1, 0)]}
        spots = [("H", n) for n in range(2, HB)] + [("Ha", HB + 1), ("Hb", HB + 1)] + \
                [("H", n) for n in range(HB + 2, 2 * HB)] + [("D", 2 * HB - 2)]
        for s in range(2):
            for k, (stage_name, layer) in zip((0, 1, 3, 5, 6, 8, 10, 11, 13), (
                    ("turn", 0), ("down", 0), ("up", 0), ("turn", 1), ("down", 1), ("up", 1),
                    ("turn", 2), ("down", 2), ("up", 2))):
                WINDOWS.setdefault(spots[k + s], []).append((stage_name, s, layer))
        STAGE_ORDER = [("load", 0)] + [(name, layer) for layer in range(LAYERS) for name in ("turn", "down", "up")]
        PAIR = [(name, s, layer) for name, layer in STAGE_ORDER for s in range(2)]
        BEHIND = 2
        LAST = []
        for n in range(len(STAGE_ORDER) + BEHIND):
            for s in range(4):
                at = n - BEHIND * (s // 2)
                if 0 <= at < len(STAGE_ORDER):
                    LAST.append((STAGE_ORDER[at][0], s, STAGE_ORDER[at][1]))
        LAST_PAIR = NW // 2 - 2

        def window_number(s, pair):
            return 2 * pair + s if s < 2 else NW - 4 + s

        def last_windows(window_part):
            for name, s, layer in LAST:
                window_part(name, s, layer, LAST_PAIR if s < 2 else 0, last=True)

        def group(part, window_part, attention_part, g, pair, following):
            for step in core:
                part(step[0], step[1], g)
                if pair is not None:
                    for w in WINDOWS.get(step, []):
                        window_part(*w, pair)
                if following is not None:
                    for a in ATTENTION.get(step, []):
                        attention_part(a, following)

        def whole(engine, part, window_part, attention_part):
            group(part, window_part, attention_part, 0, None, 1)
            with engine.Fori(1, NG - 1) as g:
                group(part, window_part, attention_part, g, g - 1, g + 1)
            group(part, window_part, attention_part, NG - 1, NG - 2, None)
            last_windows(window_part)

        @block.sync
        def _(sp):
            sp.dma_start(roles_i[:, :], roles.partition_broadcast(P)).then_inc(meta_in, 16)
            sp.dma_start(role_col_i[:, :], roles.rearrange("(b a) -> b a", a=1)).then_inc(meta_in, 16)
            sp.dma_start(code_col_i[:, :], codes.rearrange("(b a) -> b a", a=1)).then_inc(meta_in, 16)
            for n, w in enumerate((Wq, Wk, Wv, Wp)):
                sp.dma_start(raw[:, n, :, :], w.rearrange("(k p) m -> p k m", p=P)).then_inc(raw_in, 16)
            for at, n, b in ((CB1, 8, cb1), (MB1, 8, mb1), (BP, 2, bp), (CB2, 2, cb2), (MB2, 2, mb2)):
                sp.dma_start(bias_rows[at:at + n, :], b.rearrange("(j p) -> j p", p=P)).then_inc(bias_in, 16)
            n = 0
            for w, k in ((cW1, 1), (cW2, 4), (mW1, 1), (mW2, 4)):
                rows = w.rearrange("(c k p) m -> c p k m", k=k, p=P)
                for c in range(rows.shape[0]):
                    if n >= STAGES:
                        sp.wait_ge(chunk_lo, n - STAGES + 1)
                    sp.dma_start(stage[:, n % STAGES, :].rearrange("p (k m) -> p k m", k=k), rows[c])\
                        .then_inc(stage_in[n % STAGES], 16)
                    n += 1
            assert n == NCHUNK

            for layer, (wd, bd, wu, bu, gamma, beta) in enumerate(adapters):
                for k in range(VB):
                    sp.dma_start(packed_w[:, layer, :, k * KD:(k + 1) * KD], wd[:, k * P:(k + 1) * P, :])\
                        .then_inc(packed, 16)
                sp.dma_start(packed_w[:, layer, :, V:2 * V], wu).then_inc(packed, 16)
                sp.dma_start(packed_w[:, layer, :, 2 * V:2 * V + 1], bd.rearrange("r (p a) -> r p a", a=1),
                             allow_slow_non_contiguous=True)\
                    .then_inc(packed, 16)
                for n, row in enumerate((bu, gamma, beta)):
                    sp.dma_start(packed_rows[:, layer, n, :], row).then_inc(packed, 16)
            sp.wait_ge(packed, 16 * 7 * LAYERS)

            sp.wait_ge(windows_known, 1)
            sp.wait_ge(prepared, 1)
            sp.wait_ge(chunk_lo, NCHUNK)
            sp.wait_ge(fold_ready, 2)
            def load(slot, layer, which):
                sp.dma_start(slot.w[:, layer, :],
                             packed_w.rearrange("r l p m -> p (r l) m")[:, bass.ds(which, 1), :]
                             ).then_inc(slot.loaded[layer], 16)
                sp.dma_start(slot.rows[:, layer, :, :].rearrange("p n v -> p (n v)"),
                             packed_rows.rearrange("r l n v -> (r l) (n v)")[bass.ds(which, 1), :]
                             .to_broadcast([P, 3 * V])).then_inc(slot.loaded[layer], 16)

            with sp.Fori(0, LAST_PAIR + 1) as pair:
                role = [sp.value_load(window_meta[0:1, 0, bass.ds(2 * pair + s, 1)], min_val=0, max_val=ROLES - 1)
                        for s in range(2)]
                for layer in range(LAYERS):
                    for s, slot in enumerate(slots[0:2]):
                        which = role[s] * LAYERS + layer
                        sp.wait_ge(slot.layer_done[layer], PRIMED + pair)
                        load(slot, layer, which)
            sp.wait_ge(h_used, PRIMED + 2 * HB * NG)
            role = [sp.value_load(window_meta[0:1, 0, window_number(s, 0):window_number(s, 0) + 1],
                                  min_val=0, max_val=ROLES - 1) for s in (2, 3)]
            for layer in range(LAYERS):
                for s in (2, 3):
                    load(slots[s], layer, role[s - 2] * LAYERS + layer)
        LOADED = 32

        @block.gpsimd
        def _(pool):
            pool.sem_inc(window_done, PRIMED)
            pool.memset(ident[:, :], 0.0).then_inc(consts_zero, 1)
            pool.memset(ones[:, :], 1.0).then_inc(consts, 1)
            pool.iota(batch_id[:, :], [[1, B]], base=0, channel_multiplier=0,
                      allow_small_or_imprecise_dtypes=True).then_inc(consts, 1)
            pool.iota(feature_id[:, :], [[P, VB]], base=0, channel_multiplier=1,
                      allow_small_or_imprecise_dtypes=True).then_inc(consts, 1)
            pool.iota(window_id[:, :], [[1, NW]], base=0, channel_multiplier=0,
                      allow_small_or_imprecise_dtypes=True).then_inc(consts, 1)
            pool.iota(window_start8[:, :], [[WIN, WIN]], base=0, channel_multiplier=0,
                      allow_small_or_imprecise_dtypes=True).then_inc(consts, 1)
            for q in range(Q):
                pool.wait_ge(consts, 5 + 2 * q)
                pool.iota(row_in_batch[quarter(q), :], [[1, 1]], base=0, channel_multiplier=1,
                          allow_small_or_imprecise_dtypes=True).then_inc(consts, 1)
                pool.wait_ge(consts, 6 + 2 * q)
                pool.iota(slot_off[quarter(q), :], [[Q, WT]], base=q, channel_multiplier=0,
                          allow_small_or_imprecise_dtypes=True).then_inc(consts, 1)
            pool.wait_ge(consts_zero, 1)
            pool.wait_ge(consts, CONSTS - 1)
            pool.affine_select(out=ident[:, :], in_=ident[:, :], compare_op=ALU.not_equal, fill=1.0, base=0,
                               pattern=[[-1, P]], channel_multiplier=1).then_inc(consts, 1)
            pool.memset(minus_half[:, :], -0.5).then_inc(half_ready, 1)
            pool.wait_ge(rows_known, Q)

            def gather(g):
                for t in range(GT):
                    pool.indirect_dma_start(out=xr[:, t, :], out_offset=None, in_=x_rows,
                                            in_offset=bass.IndirectOffsetOnAxis(ap=row_idx[:, g * GT + t:g * GT + t + 1],
                                                                                axis=0)).then_inc(x_in, 16)

            def window_part(stage_name, s, layer, pair, last=False):
                slot = slots[s]
                if stage_name == "load":
                    pool.wait_ge(x1_ready, PRIMED + VB * (1 if s < 2 else NG))
                    pool.wait_ge(window_done, PRIMED + 2 * pair)
                    apart(pool)
                    pool.tensor_copy(slot.idx[:, :], out_idx[:, bass.ds(window_number(s, pair), 1), :]
                                     .rearrange("p a t -> p (a t)")).then_inc(slot.idx_ready, 1)
                if stage_name == "up":
                    pool.wait_ge(slot.var_ready, LAYERS * pair + layer + 1)
                    pool.tensor_tensor(slot.rstd[:, :], slot.var[:, :], minus_half[:, :], ALU.pow)\
                        .then_inc(slot.rstd_ready, 1)
                    if layer == LAYERS - 1:
                        pool.wait_ge(slot.idx_ready, pair + 1)
                        pool.wait_ge(slot.x_ready, PRIMED + LAYERS * (pair + 1))
                        apart(pool)
                        for t in range(WT):
                            pool.indirect_dma_start(out=out_rows, out_offset=bass.IndirectOffsetOnAxis(
                                ap=slot.idx[:, t:t + 1], axis=0), in_=slot.x[:, t, :], in_offset=None,
                                bounds_check=B * T - 1, oob_is_err=False).then_inc(slot.stored, 16)

            def stored(s, pair):
                pool.wait_ge(slots[s].stored, 16 * WT * (pair + 1))
                pool.sem_inc(window_done, 1)

            pool.wait_ge(half_ready, 1)
            gather(0)
            for g in range(1, NG - 1):
                pool.wait_ge(z_done, PRIMED + g)
                gather(g)

            def windows(pair, behind_middle=None):
                for w in PAIR:
                    window_part(*w, pair)
                    if w == ("up", 1, 0) and behind_middle:
                        behind_middle()
                for s in range(2):
                    stored(s, pair)

            def last_rows():
                pool.wait_ge(z_done, PRIMED + NG - 1)
                gather(NG - 1)
            windows(0, last_rows)
            with pool.Fori(1, LAST_PAIR) as pair:
                windows(pair)
            last_windows(window_part)
            for s, slot in enumerate(slots):
                pool.wait_ge(slot.stored, 16 * WT * (LAST_PAIR + 1 if s < 2 else 1))

        @block.scalar
        def _(act):
            for counter in (gelu_done, at_split):
                act.sem_inc(counter, PRIMED)
            for n in range(3):
                act.wait_ge(wT_turned, n + 1)
                act.activation(wT[:, n, :, :], two(bank[n][:, :]), ACT.Copy).then_inc(wT_copied, 1)
            act.wait_ge(bias_turned, 1)
            act.activation(bias[:, :], bank[6][:, 0:22], ACT.Copy).then_inc(bias_ready, 1)
            for n in range(2):
                act.wait_ge(folded, n + 1)
                act.activation(fold[:, n, :, :], two(bank[4 + n][:, :]), ACT.Copy).then_inc(fold_ready, 1)
            act.wait_ge(bias_ready, 1)

            def chunks(first, last):
                for c in range(first, last):
                    act.wait_ge(stage_in[c % STAGES], 16 * (c // STAGES + 1))
                    act.activation(w_hi[:, c * CHUNK:(c + 1) * CHUNK], stage[:, c % STAGES, :], ACT.Copy)\
                        .then_inc(chunk_hi, 1)

            def attention_part(stage_name, g):
                if stage_name == "X":
                    act.wait_ge(xT_turned, g + 1)
                    apart(act)
                    for vb in range(VB):
                        act.activation(xT[:, vb, bass.ts(g, GR)], bank[4 + vb][:, :], ACT.Copy).then_inc(xT_ready, 1)
                if stage_name == "Y":
                    act.wait_ge(y_done, g + 1)
                    for vb in range(VB):
                        act.activation(yz[:, vb, :], bank[4 + vb][:, :], ACT.Copy).then_inc(y_ready, 1)
                if stage_name == "S":
                    act.wait_ge(shifted_ready, g + 1)
                    act.activation(expd[:, :, :], shifted[:, :, :], ACT.Exp, scale=float(V) ** -0.5)\
                        .then_inc(exp_ready, 1)
                if stage_name == "Z":
                    act.wait_ge(z_done, PRIMED + g + 1)
                    for vb in range(VB):
                        act.activation(yz[:, vb, :], bank[4 + vb][:, :], ACT.Copy).then_inc(z_ready, 1)
                if stage_name == "A":
                    act.wait_ge(at_done, g + 1)
                    for vb in range(VB):
                        act.activation(at_hi[:, vb, :], bank[4 + vb][:, :], ACT.Identity,
                                       bias=bias[:, BP + vb:BP + vb + 1]).then_inc(at_split, 1)

            def part(step, n, g):
                if step in ("H", "Hb"):
                    b = (CB1 if n < HB else MB1) + n % HB
                    act.wait_ge(hidden_done, 2 * HB * g + n + 1)
                    act.wait_ge(h_lo_ready, PRIMED + 2 * HB * g + max(n - 1, 0))
                    act.activation(h_full[:, n % 2, :], bank[n % 2][:, :], ACT.Gelu, bias=bias[:, b:b + 1])\
                        .then_inc(gelu_done, 1)
                    act.wait_ge(gelu_done, PRIMED + 2 * HB * g + n + 1)
                    act.wait_ge(h_used, PRIMED + 2 * HB * g + max(n - 1, 0))
                    act.activation(h_hi[:, n % 2, :], h_full[:, n % 2, :], ACT.Copy).then_inc(h_hi_ready, 1)
                if step == "C":
                    for vb in range(VB):
                        act.wait_ge(cms_copied, VB * g + vb + 1)
                        act.activation(cms_hi[:, vb, :], cms[:, vb, :], ACT.Copy).then_inc(cms_split, 1)

            def window_part(stage_name, s, layer, pair, last=False):
                slot = slots[s]
                if stage_name == "load":
                    first = act.value_load(window_meta[0:1, 1, bass.ds(window_number(s, pair), 1)], min_val=0, max_val=B - WIN)
                    act.wait_ge(x1_ready, VB * NG + PRIMED if last else VB * (pair + 1) + PRIMED)
                    act.wait_ge(slot.x_ready, LAYERS * pair + PRIMED)
                    apart(act)
                    act.activation(slot.xT[:, :, :], xT[:, :, bass.ds(first * T, WR)], ACT.Copy).then_inc(slot.x_in, 1)
                if stage_name == "turn" and layer > 0:
                    act.wait_ge(slot.turned, LAYERS * pair + layer + 1)
                    act.activation(slot.xT[:, :, :], two(slot.bank[:, :]), ACT.Copy).then_inc(slot.x_in, 1)
                if stage_name == "down":
                    act.wait_ge(slot.loaded[layer], LOADED * (pair + 1))
                    act.wait_ge(slot.down_done, LAYERS * pair + layer + 1)
                    act.activation(slot.h[:, :], slot.bank[:, 0:WR], ACT.Gelu, bias=slot.w[:, layer, 2 * V:2 * V + 1])\
                        .then_inc(slot.h_ready, 1)

            chunks(0, 4)
            for a in "XYS":
                attention_part(a, 0)
            chunks(4, 8)
            for a in "ZA":
                attention_part(a, 0)
            chunks(8, NCHUNK)
            whole(act, part, window_part, attention_part)

        @block.vector
        def _(dve):
            for counter in (h_lo_ready, x1_ready, slots[0].x_ready, slots[1].x_ready,
                            slots[2].x_ready, slots[3].x_ready, *slots[0].layer_done, *slots[1].layer_done):
                dve.sem_inc(counter, PRIMED)
            link = linked(dve, route_step, 0)
            dve.wait_ge(meta_in, 48)
            dve.wait_ge(consts, CONSTS)
            role_row, key_row, onehot, scratch = (rt[:, n, :] for n in range(4))
            role_c, code_c, key_c, rank_c, neg_c = (rc[:, n:n + 1] for n in range(5))
            link(dve.tensor_copy(code_c, code_col_i[:, :]))
            link(dve.tensor_copy(role_row, roles_i[:, :]))
            link(dve.tensor_copy(role_c, role_col_i[:, :]))
            for r, neg in ((role_row, scratch), (role_c, neg_c)):
                link(dve.tensor_scalar(neg, r, 0.0, float(ROLES), ALU.is_lt, ALU.mult))
                link(dve.tensor_tensor(r, r, neg, ALU.add))
                link(dve.tensor_scalar(r, r, 0.0, float(ROLES - 1), ALU.max, ALU.min))
            link(dve.scalar_tensor_tensor(key_row, role_row, float(B), batch_id[:, :], ALU.mult, ALU.add))
            link(dve.scalar_tensor_tensor(key_c, role_c, float(B), feature_id[0:B, 0:1], ALU.mult, ALU.add))
            link(dve.tensor_scalar(scratch[0:B, :], key_row[0:B, :], key_c, None, ALU.is_lt))
            link(dve.tensor_reduce(rank_c, scratch[0:B, :], AX.X, ALU.add))
            link(dve.tensor_scalar(onehot[0:B, :], batch_id[0:B, :], rank_c, None, ALU.is_equal))
            link(dve.tensor_scalar(pick[0:B, 0:2, :].rearrange("p a b -> p (a b)"), ones[:, :],
                                   feature_id[0:B, 0:1], None, ALU.mult))
            dve.tensor_scalar(pick[0:B, 2:4, :].rearrange("p a b -> p (a b)"), ones[:, :],
                              code_c, None, ALU.mult).then_inc(sorted_onehot, 1)
            dve.wait_ge(sorted_ids, 1)
            dve.wait_ge(bias_ready, 1)
            sorted_batch, sorted_code = bank[7][:, 0:B], bank[7][:, B:2 * B]
            for q in range(Q):
                rows = slice(q * T, (q + 1) * T)
                dve.tensor_scalar(row_idx[rows, :], bank[7][rows, q:B:Q], float(T), row_in_batch[rows, :],
                                  ALU.mult, ALU.add).then_inc(rows_known, 1)
            for vb in range(VB):
                link(dve.tensor_scalar(cms_bias[:, vb, :], sorted_code, feature_id[:, vb:vb + 1],
                                       bias[:, CB2 + vb:CB2 + vb + 1], ALU.is_equal, ALU.add))
            place_row = key_row
            link(dve.tensor_scalar(place_row, sorted_batch, float(T), row_in_batch[:, :], ALU.mult, ALU.add))
            n0, n1, n2, o2, w1, w2, u1, u2 = (rs[:, n:n + 1] for n in range(8))
            for r, n in ((0, n0), (1, n1)):
                link(dve.tensor_scalar(scratch, role_row, float(r), None, ALU.is_equal))
                link(dve.tensor_reduce(n, scratch, AX.X, ALU.add))
            link(dve.tensor_tensor(o2, n0, n1, ALU.add))
            link(dve.tensor_scalar(n2, o2, -1.0, float(B), ALU.mult, ALU.add))
            for n, w in ((n0, w1), (n1, w2)):
                link(dve.tensor_scalar(scratch[:, 0:WIN], window_start8[:, :], n, None, ALU.is_lt))
                link(dve.tensor_reduce(w, scratch[:, 0:WIN], AX.X, ALU.add))
            link(dve.tensor_tensor(w2, w2, w1, ALU.add))
            link(dve.scalar_tensor_tensor(u1, w1, -float(WIN), n0, ALU.mult, ALU.add))
            link(dve.scalar_tensor_tensor(u2, w2, -float(WIN), o2, ALU.mult, ALU.add))
            link(dve.tensor_tensor(u2, u2, u1, ALU.subtract))
            in1, in2, start, end, first, role_w = (rw[:, n, 0:NW] for n in range(6))
            slot, ok, found, hit = (rw[:, n, :].rearrange("p (j t) -> p j t", t=WT) for n in range(6, 10))
            link(dve.tensor_scalar(in1, window_id[:, :], w1, None, ALU.is_ge))
            link(dve.tensor_scalar(in2, window_id[:, :], w2, None, ALU.is_ge))
            link(dve.tensor_tensor(role_w, in1, in2, ALU.add))
            link(dve.tensor_scalar(start, window_id[:, :], float(WIN), None, ALU.mult))
            link(dve.scalar_tensor_tensor(start, in1, u1, start, ALU.mult, ALU.add))
            link(dve.scalar_tensor_tensor(start, in2, u2, start, ALU.mult, ALU.add))
            link(dve.tensor_scalar(end, in1, n1, n0, ALU.mult, ALU.add))
            link(dve.scalar_tensor_tensor(end, in2, n2, end, ALU.mult, ALU.add))
            link(dve.tensor_scalar(first, start, float(B - WIN), None, ALU.min))
            link(dve.tensor_copy(window_meta[:, 0, :], role_w))
            link(dve.tensor_copy(window_meta[:, 1, :], first))
            wide = [P, NW, WT]
            link(dve.tensor_tensor(slot, first.unsqueeze(2).to_broadcast(wide),
                                   slot_off[:, :].unsqueeze(1).to_broadcast(wide), ALU.add))
            link(dve.tensor_tensor(ok, slot, start.unsqueeze(2).to_broadcast(wide), ALU.is_ge))
            link(dve.tensor_tensor(hit, slot, end.unsqueeze(2).to_broadcast(wide), ALU.is_lt))
            link(dve.tensor_tensor(ok, ok, hit, ALU.mult))
            flat = [P, NW * WT, B]
            link(dve.tensor_tensor(pick[:, :, :], rw[:, 6, :].unsqueeze(2).to_broadcast(flat),
                                   batch_id[:, :].unsqueeze(1).to_broadcast(flat), ALU.is_equal))
            link(dve.tensor_tensor(pick[:, :, :], pick[:, :, :], place_row.unsqueeze(1).to_broadcast(flat), ALU.mult))
            link(dve.tensor_reduce(rw[:, 8, :], pick[:, :, :], AX.X, ALU.add))
            link(dve.scalar_tensor_tensor(found, ok, -float(OUT_OF_RANGE), found, ALU.mult, ALU.add))
            dve.tensor_scalar(out_idx[:, :, :], found, float(OUT_OF_RANGE), None, ALU.add).then_inc(windows_known, 1)
            dve.memset(pd[:, :, :], 0.0).then_inc(pd_clear, 1)
            dve.sem_inc(prepared, 1)

            def chunks(first, last):
                for c in range(first, last):
                    cols = slice(c * CHUNK, (c + 1) * CHUNK)
                    dve.wait_ge(chunk_hi, c + 1)
                    dve.tensor_tensor(w_lo[:, cols], stage[:, c % STAGES, :], w_hi[:, cols].bitcast(F32),
                                      ALU.subtract).then_inc(chunk_lo, 1)

            def attention_part(stage_name, g):
                if stage_name == "S":
                    link = linked(dve, softmax_step, SOFTMAX_STEPS * g)
                    dve.wait_ge(scores_done, g + 1)
                    own = [bank[4][quarter(q), :].rearrange("p (i c) -> p i c", c=P)[:, :, quarter(q)]
                           for q in range(Q)]
                    for q in range(Q):
                        ins = dve.tensor_reduce(row_max[quarter(q), :], own[q], AX.X, ALU.max)
                    link(ins)
                    for q in range(Q):
                        ins = dve.tensor_tensor(shifted[quarter(q), :, :], own[q],
                                                row_max[quarter(q), :].unsqueeze(2).to_broadcast([T, GT, T]),
                                                ALU.subtract)
                    ins.then_inc(shifted_ready, 1)
                if stage_name == "P":
                    link = linked(dve, softmax_step, SOFTMAX_STEPS * g + 1)
                    dve.wait_ge(exp_ready, g + 1)
                    link(dve.tensor_reduce(row_sum[:, 0, :], expd[:, :, :], AX.X, ALU.add))
                    link(dve.reciprocal(row_sum[:, 1, :], row_sum[:, 0, :]))
                    link(dve.tensor_tensor(prob[:, :, :], expd[:, :, :],
                                           row_sum[:, 1, :].unsqueeze(2).to_broadcast([P, GT, T]), ALU.mult))
                    link(dve.transpose(probT[:, :, :], prob[:, :, :]))
                    for q in range(Q):
                        ins = dve.tensor_copy(pd[quarter(q), :, quarter(q)], probT[quarter(q), :, :])
                    ins.then_inc(pd_ready, 1)
                if stage_name == "A":
                    for vb in range(VB):
                        dve.wait_ge(at_split, PRIMED + 2 * VB * g + VB)
                        dve.scalar_tensor_tensor(at_lo[:, vb, :], bank[4 + vb][:, :], bias[:, BP + vb:BP + vb + 1],
                                                 at_hi[:, vb, :].bitcast(F32), ALU.add, ALU.subtract)\
                            .then_inc(at_split, 1)

            def part(step, n, g):
                if step in ("H", "Hb"):
                    dve.wait_ge(h_hi_ready, 2 * HB * g + n + 1)
                    dve.tensor_tensor(h_lo[:, n % 2, :], h_full[:, n % 2, :], h_hi[:, n % 2, :].bitcast(F32),
                                      ALU.subtract).then_inc(h_lo_ready, 1)
                if step == "C":
                    dve.wait_ge(h_used, PRIMED + 2 * HB * g + HB)
                    for vb in range(VB):
                        dve.tensor_tensor(
                            cms[:, vb, :].rearrange("p (b t) -> p b t", t=T),
                            bank[2 + vb][:, :].rearrange("p (b t) -> p b t", t=T),
                            cms_bias[:, vb, bass.ts(g, GB)].unsqueeze(2).to_broadcast([P, GB, T]), ALU.add)\
                            .then_inc(cms_copied, 1)
                    for vb in range(VB):
                        dve.wait_ge(cms_split, 2 * VB * g + VB)
                        dve.tensor_tensor(cms_lo[:, vb, :], cms[:, vb, :], cms_hi[:, vb, :].bitcast(F32),
                                          ALU.subtract).then_inc(cms_split, 1)
                    for vb in range(VB):
                        dve.tensor_tensor(xT[:, vb, bass.ts(g, GR)], xT[:, vb, bass.ts(g, GR)], cms[:, vb, :],
                                          ALU.add).then_inc(base_ready, 1)
                if step == "F":
                    dve.wait_ge(h_used, PRIMED + 2 * HB * (g + 1))
                    dve.wait_ge(base_ready, VB * (g + 1))
                    for vb in range(VB):
                        dve.scalar_tensor_tensor(cms[:, vb, :], bank[2 + vb][:, :], bias[:, MB2 + vb:MB2 + vb + 1],
                                                 xT[:, vb, bass.ts(g, GR)], ALU.add, ALU.add).then_inc(mod_summed, 1)
                    for vb in range(VB):
                        dve.wait_ge(mod_summed, VB * g + vb + 1)
                        dve.tensor_scalar(xT[:, vb, bass.ts(g, GR)], cms[:, vb, :], 0.0, 1.0, ALU.max, ALU.min)\
                            .then_inc(x1_ready, 1)

            def window_part(stage_name, s, layer, pair, last=False):
                slot = slots[s]

                def row(n, lay):
                    return slot.rows[:, lay, n, :].unsqueeze(1).to_broadcast([P, WT, V])
                if stage_name == "turn" and layer == 0:
                    dve.wait_ge(slot.loaded[0], LOADED * (pair + 1))
                    dve.wait_ge(slot.turned, LAYERS * pair + 1)
                    dve.tensor_tensor(slot.y[:, :, :], two(slot.bank[:, :]), row(0, 0), ALU.add)\
                        .then_inc(slot.y_ready, 1)
                if stage_name == "up":
                    link = linked(dve, slot.norm_step, NORM_STEPS * (LAYERS * pair + layer))
                    if layer < LAYERS - 1:
                        dve.wait_ge(slot.loaded[layer + 1], LOADED * (pair + 1))
                    dve.wait_ge(slot.up_done, LAYERS * pair + layer + 1)
                    dve.wait_ge(slot.y_ready, LAYERS * pair + layer + 1)
                    link(dve.tensor_tensor(slot.y[:, :, :], two(slot.bank[:, :]), slot.y[:, :, :], ALU.add))
                    for t in range(WT):
                        ins = dve.bn_stats(slot.stats[:, t, :], slot.y[:, t, :])
                    link(ins)
                    apart(dve)
                    for t in range(WT):
                        ins = dve.bn_aggr(slot.moments[:, t, :], slot.stats[:, t, :])
                    link(ins)
                    dve.tensor_scalar(slot.var[:, :], slot.moments[:, :, 1:2].rearrange("p t a -> p (t a)"), EPS, None,
                                      ALU.add).then_inc(slot.var_ready, 1)
                    for t in range(WT):
                        ins = dve.scalar_tensor_tensor(slot.y[:, t, :], slot.y[:, t, :], slot.moments[:, t, 0:1],
                                                       slot.rows[:, layer, 1, :], ALU.subtract, ALU.mult)
                    link(ins)
                    dve.wait_ge(slot.rstd_ready, LAYERS * pair + layer + 1)
                    for t in range(WT):
                        ins = dve.scalar_tensor_tensor(slot.x[:, t, :], slot.y[:, t, :], slot.rstd[:, t:t + 1],
                                                       slot.rows[:, layer, 2, :], ALU.mult, ALU.add)
                    ins.then_inc(slot.x_ready, 1)
                    dve.wait_ge(slot.x_ready, PRIMED + LAYERS * pair + layer + 1)
                    if s < 2:
                        dve.sem_inc(slot.layer_done[layer], 1)
                    if layer < LAYERS - 1:
                        dve.tensor_tensor(slot.y[:, :, :], slot.x[:, :, :], row(0, layer + 1), ALU.add)\
                            .then_inc(slot.y_ready, 1)

            chunks(0, 4)
            dve.wait_ge(pd_clear, 1)
            attention_part("S", 0)
            attention_part("P", 0)
            chunks(4, 8)
            attention_part("A", 0)
            chunks(8, NCHUNK)
            whole(dve, part, window_part, attention_part)

        @block.tensor
        def _(pe):
            for counter in (z_done, h_used):
                pe.sem_inc(counter, PRIMED)
            pe.wait_ge(consts, CONSTS)
            pe.wait_ge(raw_in, 16 * 4)
            for n in range(3):
                for eb in range(VB):
                    for db in range(VB):
                        ins = pe.transpose(bank[n][:, eb * V + db * P:eb * V + (db + 1) * P],
                                           raw[:, n, db, eb * P:(eb + 1) * P], ident[:, :])
                ins.then_inc(wT_turned, 1)
            pe.wait_ge(bias_in, 16 * 5)
            pe.transpose(bank[6][:, 0:22], bias_rows[:, :], ident[0:22, 0:22]).then_inc(bias_turned, 1)
            pe.wait_ge(sorted_onehot, 1)
            for n in range(2):
                ins = pe.matmul(bank[7][:, n * B:(n + 1) * B], pick[0:B, 2 * n:2 * n + 2, :].rearrange("p a b -> p (a b)"),
                                rt[0:B, 2, :], start=True, stop=True)
            ins.then_inc(sorted_ids, 1)
            for n, (lhs, rhs) in enumerate(((wT[:, 0], wT[:, 1]), (wT[:, 2], raw[:, 3]))):
                pe.wait_ge(wT_copied, 2 + n)
                for db in range(VB):
                    for eb in range(VB):
                        ins = pe.matmul(bank[4 + n][:, db * V:(db + 1) * V], lhs[:, eb, db * P:(db + 1) * P],
                                        rhs[:, eb, :], start=(eb == 0), stop=(eb == VB - 1))
                ins.then_inc(folded, 1)
            pe.wait_ge(fold_ready, 2)

            def attention_part(stage_name, g):
                first = g * GR
                if stage_name == "X":
                    pe.wait_ge(x_in, 16 * GT * (g + 1))
                    pe.wait_ge(at_split, PRIMED + 2 * VB * g)
                    for vb in range(VB):
                        for i in range(GT):
                            ins = pe.transpose(bank[4 + vb][:, i * P:(i + 1) * P], xr[:, i, vb * P:(vb + 1) * P],
                                               ident[:, :])
                    ins.then_inc(xT_turned, 1)
                if stage_name == "Y":
                    pe.wait_ge(xT_ready, VB * (g + 1))
                    for ob in range(VB):
                        for k in range(VB):
                            ins = pe.matmul(bank[4 + ob][:, :], fold[:, 0, k, ob * P:(ob + 1) * P],
                                            xT[:, k, bass.ds(first, GR)], start=(k == 0), stop=(k == VB - 1))
                    ins.then_inc(y_done, 1)
                if stage_name == "S":
                    pe.wait_ge(y_ready, VB * (g + 1))
                    for i in range(GT):
                        cols = slice(i * P, (i + 1) * P)
                        for k in range(VB):
                            ins = pe.matmul(bank[4][:, cols], yz[:, k, cols], xT[:, k, bass.ds(first + i * P, P)],
                                            start=(k == 0), stop=(k == VB - 1))
                    ins.then_inc(scores_done, 1)
                if stage_name == "Z":
                    pe.wait_ge(pd_ready, g + 1)
                    for vb in range(VB):
                        for i in range(GT):
                            ins = pe.matmul(bank[4 + vb][:, i * P:(i + 1) * P], xr[:, i, vb * P:(vb + 1) * P],
                                            pd[:, i, :], start=True, stop=True)
                    ins.then_inc(z_done, 1)
                if stage_name == "A":
                    pe.wait_ge(z_ready, VB * (g + 1))
                    for ob in range(VB):
                        for k in range(VB):
                            ins = pe.matmul(bank[4 + ob][:, :], fold[:, 1, k, ob * P:(ob + 1) * P], yz[:, k, :],
                                            start=(k == 0), stop=(k == VB - 1))
                    ins.then_inc(at_done, 1)

            def part(step, n, g):
                if step in ("H", "Ha", "Hb"):
                    w, j = (CW1, n) if n < HB else (MW1, n - HB)
                    k_all = VB if n < HB else 2 * VB
                    ks = range(VB) if step == "Ha" else range(VB, 2 * VB) if step == "Hb" else range(k_all)
                    if step != "Hb":
                        pe.wait_ge(gelu_done, PRIMED + 2 * HB * g + max(n - 1, 0))
                    if n == 0:
                        pe.wait_ge(at_split, PRIMED + 2 * VB * (g + 1))
                    if isinstance(g, int) and g == 0 and n in (0, HB):
                        pe.wait_ge(chunk_lo, 2 if n == 0 else 8)
                    if n == HB and step == "Hb":
                        pe.wait_ge(cms_split, 2 * VB * (g + 1))
                    for k in ks:
                        cols = slice(w + k * H + j * P, w + k * H + (j + 1) * P)
                        r_hi, r_lo = ((at_hi[:, k, :], at_lo[:, k, :]) if k < VB
                                      else (cms_hi[:, k - VB, :], cms_lo[:, k - VB, :]))
                        ins = mm3(pe, bank[n % 2][:, :], w_hi[:, cols], w_lo[:, cols], r_hi, r_lo,
                                  k == 0, k == k_all - 1)
                    if step != "Ha":
                        ins.then_inc(hidden_done, 1)
                if step == "D":
                    w, j = (CW2, n) if n < HB else (MW2, n - HB)
                    pe.wait_ge(h_hi_ready, 2 * HB * g + n + 1)
                    if n == 0 and not (isinstance(g, int) and g == 0):
                        pe.wait_ge(mod_summed, VB * g)
                    if isinstance(g, int) and g == 0 and n in (0, HB):
                        pe.wait_ge(chunk_lo, 4 if n == 0 else NCHUNK)
                    for ob in range(VB):
                        cols = slice(w + j * V + ob * P, w + j * V + (ob + 1) * P)
                        pe.matmul(bank[2 + ob][:, :], w_hi[:, cols], h_hi[:, n % 2, :], start=(j == 0), stop=False)
                        pe.matmul(bank[2 + ob][:, :], w_lo[:, cols], h_hi[:, n % 2, :], start=False, stop=False)
                    pe.wait_ge(h_lo_ready, PRIMED + 2 * HB * g + n + 1)
                    for ob in range(VB):
                        cols = slice(w + j * V + ob * P, w + j * V + (ob + 1) * P)
                        ins = pe.matmul(bank[2 + ob][:, :], w_hi[:, cols], h_lo[:, n % 2, :], start=False,
                                        stop=(j == HB - 1))
                    ins.then_inc(h_used, 1)

            def window_part(stage_name, s, layer, pair, last=False):
                slot = slots[s]
                if stage_name == "turn" and layer == 0:
                    pe.wait_ge(slot.x_in, LAYERS * pair + 1)
                    for t in range(WT):
                        for vb in range(VB):
                            ins = pe.transpose(slot.bank[:, t * V + vb * P:t * V + (vb + 1) * P],
                                               slot.xT[:, vb, t * P:(t + 1) * P], ident[:, :])
                    ins.then_inc(slot.turned, 1)
                if stage_name == "turn" and layer > 0:
                    pe.wait_ge(slot.x_ready, PRIMED + LAYERS * pair + layer)
                    for vb in range(VB):
                        for t in range(WT):
                            ins = pe.transpose(slot.bank[:, vb * WR + t * P:vb * WR + (t + 1) * P],
                                               slot.x[:, t, vb * P:(vb + 1) * P], ident[:, :])
                    ins.then_inc(slot.turned, 1)
                if stage_name == "down":
                    pe.wait_ge(slot.loaded[layer], LOADED * (pair + 1))
                    if layer == 0:
                        pe.wait_ge(slot.y_ready, LAYERS * pair + 1)
                    pe.wait_ge(slot.x_in, LAYERS * pair + layer + 1)
                    for vb in range(VB):
                        ins = pe.matmul(slot.bank[:, 0:WR], slot.w[:, layer, vb * KD:(vb + 1) * KD], slot.xT[:, vb, :],
                                        start=(vb == 0), stop=(vb == VB - 1))
                    ins.then_inc(slot.down_done, 1)
                if stage_name == "up":
                    pe.wait_ge(slot.h_ready, LAYERS * pair + layer + 1)
                    for t in range(WT):
                        ins = pe.matmul(slot.bank[:, t * V:(t + 1) * V], slot.h[:, t * P:(t + 1) * P],
                                        slot.w[:, layer, V:2 * V], start=True, stop=True)
                    ins.then_inc(slot.up_done, 1)

            for a in "XYSZA":
                attention_part(a, 0)
            whole(pe, part, window_part, attention_part)


_ADAPTER = [("W_down", "b_down", "W_up", "b_up", "gamma", "beta"),
            ("W_down", "b_down", "W_up", "b_up", "ln_w", "ln_b"),
            ("W_down", "b_down", "W_up", "b_up", "ln_w", "ln_b")]
_INS = ["x", "itok_B_17_1546", "itok_B_1_2"] + ["L0_cond_" + n for n in (
    "Wq", "Wk", "Wv", "Wp", "bp", "cW1", "cb1", "cW2", "cb2", "mW1", "mb1", "mW2", "mb2")]
_INS_ADAPTERS = [[f"L{i + 1}_cond_{n}" for n in names] for i, names in enumerate(_ADAPTER)]


def kernel(**inputs):
    import numpy as _np
    import concourse.bacc as _bacc
    from concourse import mybir as _mybir
    from concourse.bass_utils import run_bass_kernel_spmd as _run

    nc = _bacc.Bacc("TRN2", target_bir_lowering=False, num_devices=1)
    arrays = {}

    def declare(name):
        a = _np.ascontiguousarray(inputs[name])
        arrays[f"in_{name}"] = a
        return nc.dram_tensor(f"in_{name}", a.shape, _mybir.dt.from_np(a.dtype), kind="ExternalInput").ap()

    args = [declare(n) for n in _INS]
    adapters = [[declare(n) for n in names] for names in _INS_ADAPTERS]
    out = nc.dram_tensor("out_0", (64, 32, 256), _mybir.dt.float32, kind="ExternalOutput").ap()
    build(nc, *args, adapters, out)
    r = _run(nc, [arrays], core_ids=[0])
    return r.results[0]["out_0"]
```

```python
from contextlib import ExitStack

import concourse.bass as bass
from concourse import mybir

F32 = mybir.dt.float32
F32R = mybir.dt.float32r
I32 = mybir.dt.int32
ALU = mybir.AluOpType
ACT = mybir.ActivationFunctionType
AX = mybir.AxisListType

P = 128
B, T, V = 64, 32, 256
H = 4 * V
KD = 128
ROLES, LAYERS = 3, 3
VB = V // P
HB = H // P
Q = P // T
GT = 4
GR = GT * P
GB = GT * Q
NG = B // GB
WIN = 8
WR = WIN * T
WT = WR // P
NW = B // WIN + ROLES - 1
EPS = 1e-5
OUT_OF_RANGE = 4096

CW1, CW2, MW1, MW2 = 0, 2 * H, 4 * H, 8 * H
CHUNK = 1024
NCHUNK = 10
STAGES = 6


def build(nc, x, codes, roles, Wq, Wk, Wv, Wp, bp, cW1, cb1, cW2, cb2, mW1, mb1, mW2, mb2, adapters, out):
    x_rows = x.rearrange("b t v -> (b t) v")
    out_rows = out.rearrange("b t v -> (b t) v")

    with ExitStack() as ctx:
        def sb(name, shape, dt=F32, scope=ctx):
            return scope.enter_context(nc.sbuf_tensor(name, shape, dt))

        def sem(name):
            return ctx.enter_context(nc.semaphore(name))

        bank = [ctx.enter_context(nc.psum_tensor(f"bank{i}", [P, GR], F32)) for i in range(8)]

        ident = sb("ident", [P, P])
        ones = sb("ones", [B, P])
        batch_id = sb("batch_id", [P, B])
        feature_id = sb("feature_id", [P, VB])
        row_in_batch = sb("row_in_batch", [P, 1])
        window_id = sb("window_id", [P, NW])
        window_start8 = sb("window_start8", [P, WIN])
        slot_off = sb("slot_off", [P, WT])
        roles_i = sb("roles_i", [P, B], I32)
        role_col_i = sb("role_col_i", [B, 1], I32)
        code_col_i = sb("code_col_i", [B, 1], I32)
        row_idx = sb("row_idx", [P, NG * GT], I32)
        out_idx = sb("out_idx", [P, NW, WT], I32)
        window_meta = sb("window_meta", [P, 2, NW], I32)
        cms_bias = sb("cms_bias", [P, VB, B])
        bias_rows = sb("bias_rows", [22, P])
        bias = sb("bias", [P, 22])
        FIRST_CONSTS, CONSTS = 4, Q + 2
        CB1, MB1, BP, CB2, MB2 = 0, 8, 16, 18, 20

        packed_w = nc.dram_tensor("packed_w", (ROLES, LAYERS, P, 2 * V + 1), F32).ap()
        packed_rows = nc.dram_tensor("packed_rows", (ROLES, LAYERS, 3, V), F32).ap()

        fold = sb("fold", [P, 2, VB, V])
        xT = sb("xT", [P, VB, NG * GR])

        xr = sb("xr", [P, GT, V])
        yz = sb("yz", [P, VB, GR])
        pd = sb("pd", [P, GT, P])
        row_max = sb("row_max", [P, GT])
        shifted = sb("shifted", [P, GT, T])
        expd = sb("expd", [P, GT, T])
        row_sum = sb("row_sum", [P, 2, GT])
        prob = sb("prob", [P, GT, T])
        probT = sb("probT", [P, GT, T])
        at_hi = sb("at_hi", [P, VB, GR], F32R)
        at_lo = sb("at_lo", [P, VB, GR], F32R)

        def adapter_weights(n, scope):
            return (sb(f"adapter_w{n}", [P, LAYERS, 2 * V + 1], scope=scope),
                    sb(f"adapter_rows{n}", [P, LAYERS, 3, V], scope=scope))

        class Slot:
            def __init__(self, n, scope, weights):
                self.w, self.rows = weights
                self.xT = sb(f"window_xT{n}", [P, VB, WR], scope=scope)
                self.y = sb(f"window_y{n}", [P, WT, V], scope=scope)
                self.h = sb(f"window_h{n}", [P, WR], scope=scope)
                self.x = sb(f"window_x{n}", [P, WT, V], scope=scope)
                self.stats = sb(f"stats{n}", [P, WT, 6], scope=scope)
                self.moments = sb(f"moments{n}", [P, WT, 2], scope=scope)
                self.var = sb(f"var_eps{n}", [P, WT], scope=scope)
                self.rstd = sb(f"rstd{n}", [P, WT], scope=scope)
                self.idx = sb(f"store_idx{n}", [P, WT], I32, scope=scope)
                self.bank = bank[(6, 7, 4, 5)[n]]
                self.sum_bank = bank[n]
                self.loaded = [sem(f"adapter_loaded{n}_{layer}") for layer in range(LAYERS)]
                self.x_in = sem(f"window_x_in{n}")
                self.turned = sem(f"window_turned{n}")
                self.y_ready = sem(f"window_y_ready{n}")
                self.down_done = sem(f"down_done{n}")
                self.h_ready = sem(f"window_h_ready{n}")
                self.up_done = sem(f"up_done{n}")
                self.norm_step = sem(f"norm_step{n}")
                self.var_ready = sem(f"var_ready{n}")
                self.rstd_ready = sem(f"rstd_ready{n}")
                self.x_ready = sem(f"window_x_ready{n}")
                self.layer_done = [sem(f"layer_done{n}_{layer}") for layer in range(LAYERS)]
                self.idx_ready = sem(f"idx_ready{n}")
                self.stored = sem(f"stored{n}")

        packed = sem("packed")
        minus_half = sb("minus_half", [P, WT])

        with ExitStack() as scope:
            stage = sb("stage", [P, STAGES, CHUNK], scope=scope)
            raw = sb("raw", [P, 4, VB, V], scope=scope)
            wT = sb("wT", [P, 3, VB, V], scope=scope)
            rt = sb("rt", [P, 4, B], scope=scope)
            rc = sb("rc", [B, 8], scope=scope)
            rs = sb("rs", [P, 32], scope=scope)
            rw = sb("rw", [P, 10, NW * WT], scope=scope)
            pick = sb("pick", [P, NW * WT, B], scope=scope)
        slots = [Slot(n, ctx, adapter_weights(n, ctx)) for n in range(2)]
        h_full = sb("h_full", [P, 2, GR])
        h_hi = sb("h_hi", [P, 2, GR], F32R)
        h_lo = sb("h_lo", [P, 2, GR], F32R)
        cms = sb("cms", [P, VB, GR])
        cms_hi = sb("cms_hi", [P, VB, GR], F32R)
        cms_lo = sb("cms_lo", [P, VB, GR], F32R)
        with ExitStack() as scope:
            c_hi = sb("c_hi", [P, MW1], F32R, scope)
            c_lo = sb("c_lo", [P, MW1], F32R, scope)
            m_hi = sb("m_hi", [P, NCHUNK * CHUNK - MW1], F32R, scope)
            m_lo = sb("m_lo", [P, NCHUNK * CHUNK - MW1], F32R, scope)
        last_w = [adapter_weights(n, ctx) for n in (2, 3)]
        slots += [Slot(n, ctx, last_w[n - 2]) for n in (2, 3)]

        def high(cols):
            return c_hi[:, cols] if cols.stop <= MW1 else m_hi[:, cols.start - MW1:cols.stop - MW1]

        def low(cols):
            return c_lo[:, cols] if cols.stop <= MW1 else m_lo[:, cols.start - MW1:cols.stop - MW1]

        meta_in = sem("meta_in")
        bias_in = sem("bias_in")
        raw_in = sem("raw_in")
        consts = sem("consts")
        first_consts = sem("first_consts")
        row_ids = sem("row_ids")
        consts_zero = sem("consts_zero")
        route_step = sem("route_step")
        sorted_onehot = sem("sorted_onehot")
        sorted_ids = sem("sorted_ids")
        rows_known = sem("rows_known")
        windows_known = sem("windows_known")
        bias_turned = sem("bias_turned")
        bias_ready = sem("bias_ready")
        wT_turned = sem("wT_turned")
        wT_copied = sem("wT_copied")
        folded = sem("folded")
        fold_ready = sem("fold_ready")
        chunk_hi = sem("chunk_hi")
        chunk_lo = sem("chunk_lo")
        prepared = sem("prepared")
        x_in = sem("x_in")
        xT_turned = sem("xT_turned")
        xT_ready = sem("xT_ready")
        y_done = sem("y_done")
        y_ready = sem("y_ready")
        scores_done = sem("scores_done")
        softmax_step = sem("softmax_step")
        shifted_ready = sem("shifted_ready")
        exp_ready = sem("exp_ready")
        pd_clear = sem("pd_clear")
        pd_ready = sem("pd_ready")
        z_done = sem("z_done")
        z_ready = sem("z_ready")
        at_done = sem("at_done")
        at_split = sem("at_split")
        hidden_done = sem("hidden_done")
        gelu_done = sem("gelu_done")
        h_hi_ready = sem("h_hi_ready")
        h_lo_ready = sem("h_lo_ready")
        h_used = sem("h_used")
        cms_copied = sem("cms_copied")
        cms_split = sem("cms_split")
        base_ready = sem("base_ready")
        mod_summed = sem("mod_summed")
        x1_ready = sem("x1_ready")
        window_done = sem("window_done")
        half_ready = sem("half_ready")
        waited = sem("waited")
        stage_in = [sem(f"stage_in{s}") for s in range(STAGES)]

        block = ctx.enter_context(nc.Block())

        def mm3(pe, o, w_hi_ap, w_lo_ap, r_hi_ap, r_lo_ap, first, last):
            pe.matmul(o, w_hi_ap, r_hi_ap, start=first, stop=False)
            pe.matmul(o, w_lo_ap, r_hi_ap, start=False, stop=False)
            return pe.matmul(o, w_hi_ap, r_lo_ap, start=False, stop=last)

        def linked(engine, counter, base):
            n = [0]

            def link(ins):
                n[0] += 1
                ins.then_inc(counter, 1)
                engine.wait_ge(counter, base + n[0])
            return link

        def apart(engine):
            engine.sem_inc(waited, 1)

        def quarter(q):
            return slice(q * T, (q + 1) * T)

        def two(ap):
            return ap.rearrange("p (k m) -> p k m", k=2)

        PRIMED = 1
        SOFTMAX_STEPS, NORM_STEPS = 5, 4

        core = [("H", 0), ("H", 1)]
        for n in range(HB - 2):
            core += [("D", n), ("H", n + 2)]
        core += [("D", HB - 2), ("Ha", HB), ("D", HB - 1), ("C", 0), ("Ha", HB + 1), ("Hb", HB), ("Hb", HB + 1)]
        for n in range(HB, 2 * HB - 2):
            core += [("D", n), ("H", n + 2)]
        core += [("D", 2 * HB - 2), ("D", 2 * HB - 1), ("F", 0)]
        ATTENTION = {("H", 2): ["X"], ("H", 3): ["Y"], ("H", 4): ["S"], ("H", 5): ["P"], ("Ha", HB + 1): ["Z"],
                     ("H", 2 * HB - 1): ["A", "B"]}
        WINDOWS = {("H", 1): [("load", 0, 0), ("load", 1, 0)]}
        spots = [("H", n) for n in range(2, HB)] + [("Ha", HB + 1), ("Hb", HB + 1)] + \
                [("H", n) for n in range(HB + 2, 2 * HB)] + [("D", 2 * HB - 2), ("F", 0)]
        for s in range(2):
            for k, (stage_name, layer) in zip(((0, 1, 2, 3, 4, 6, 7, 8, 9, 10, 11, 12),
                                            (1, 2, 3, 4, 6, 7, 8, 9, 10, 11, 12, 13))[s], (
                    (name, layer) for layer in range(LAYERS) for name in ("turn", "down", "up", "norm"))):
                WINDOWS.setdefault(spots[k], []).append((stage_name, s, layer))
        STAGE_ORDER = [("load", 0)] + [(name, layer) for layer in range(LAYERS) for name in ("turn", "down", "up", "norm")]
        PAIR = [(name, s, layer) for name, layer in STAGE_ORDER for s in range(2)]
        BEHIND = 1
        LAST = [("load", s, 0) for s in range(4)]
        for n in range(1, len(STAGE_ORDER) + BEHIND):
            for s in range(4):
                at = n - BEHIND * (s // 2)
                if 1 <= at < len(STAGE_ORDER):
                    LAST.append((STAGE_ORDER[at][0], s, STAGE_ORDER[at][1]))
        LAST_PAIR = NW // 2 - 2

        def window_number(s, pair):
            return 2 * pair + s if s < 2 else NW - 4 + s

        def last_windows(window_part):
            for name, s, layer in LAST:
                window_part(name, s, layer, LAST_PAIR if s < 2 else 0, last=True)

        def group(part, window_part, attention_part, g, pair, following):
            for step in core:
                part(step[0], step[1], g)
                if pair is not None:
                    for w in WINDOWS.get(step, []):
                        window_part(*w, pair)
                if following is not None:
                    for a in ATTENTION.get(step, []):
                        attention_part(a, following)

        def whole(engine, part, window_part, attention_part):
            group(part, window_part, attention_part, 0, None, 1)
            with engine.Fori(1, NG - 1) as g:
                group(part, window_part, attention_part, g, g - 1, g + 1)
            group(part, window_part, attention_part, NG - 1, NG - 2, None)
            last_windows(window_part)

        @block.sync
        def _(sp):
            sp.dma_start(roles_i[:, :], roles.partition_broadcast(P)).then_inc(meta_in, 16)
            sp.dma_start(role_col_i[:, :], roles.rearrange("(b a) -> b a", a=1)).then_inc(meta_in, 16)
            sp.dma_start(code_col_i[:, :], codes.rearrange("(b a) -> b a", a=1)).then_inc(meta_in, 16)
            for n, w in enumerate((Wq, Wk, Wv, Wp)):
                sp.dma_start(raw[:, n, :, :], w.rearrange("(k p) m -> p k m", p=P)).then_inc(raw_in, 16)
            for at, n, b in ((CB1, 8, cb1), (MB1, 8, mb1), (BP, 2, bp), (CB2, 2, cb2), (MB2, 2, mb2)):
                sp.dma_start(bias_rows[at:at + n, :], b.rearrange("(j p) -> j p", p=P)).then_inc(bias_in, 16)
            sp.wait_ge(x_in, 16 * GT)
            n = 0
            for w, k in ((cW1, 1), (cW2, 4), (mW1, 1), (mW2, 4)):
                rows = w.rearrange("(c k p) m -> c p k m", k=k, p=P)
                for c in range(rows.shape[0]):
                    if n >= STAGES:
                        sp.wait_ge(chunk_lo, n - STAGES + 1)
                    sp.dma_start(stage[:, n % STAGES, :].rearrange("p (k m) -> p k m", k=k), rows[c])\
                        .then_inc(stage_in[n % STAGES], 16)
                    n += 1
            assert n == NCHUNK

            for layer, (wd, bd, wu, bu, gamma, beta) in enumerate(adapters):
                for k in range(VB):
                    sp.dma_start(packed_w[:, layer, :, k * KD:(k + 1) * KD], wd[:, k * P:(k + 1) * P, :])\
                        .then_inc(packed, 16)
                sp.dma_start(packed_w[:, layer, :, V:2 * V], wu).then_inc(packed, 16)
                sp.dma_start(packed_w[:, layer, :, 2 * V:2 * V + 1], bd.rearrange("r (p a) -> r p a", a=1),
                             allow_slow_non_contiguous=True)\
                    .then_inc(packed, 16)
                for n, row in enumerate((bu, gamma, beta)):
                    sp.dma_start(packed_rows[:, layer, n, :], row).then_inc(packed, 16)
            sp.wait_ge(packed, 16 * 7 * LAYERS)

            sp.wait_ge(windows_known, 1)
            sp.wait_ge(prepared, 1)
            sp.wait_ge(chunk_lo, NCHUNK)
            sp.wait_ge(fold_ready, 2)
            def load(slot, layer, which):
                sp.dma_start(slot.w[:, layer, :],
                             packed_w.rearrange("r l p m -> p (r l) m")[:, bass.ds(which, 1), :]
                             ).then_inc(slot.loaded[layer], 16)
                sp.dma_start(slot.rows[:, layer, :, :].rearrange("p n v -> p (n v)"),
                             packed_rows.rearrange("r l n v -> (r l) (n v)")[bass.ds(which, 1), :]
                             .to_broadcast([P, 3 * V])).then_inc(slot.loaded[layer], 16)

            def load_pair(pair):
                role = [sp.value_load(window_meta[0:1, 0, bass.ds(2 * pair + s, 1)], min_val=0, max_val=ROLES - 1)
                        for s in range(2)]
                for layer in range(LAYERS):
                    for s, slot in enumerate(slots[0:2]):
                        which = role[s] * LAYERS + layer
                        sp.wait_ge(slot.layer_done[layer], PRIMED + pair)
                        load(slot, layer, which)

            with sp.Fori(0, LAST_PAIR) as pair:
                load_pair(pair)
            sp.wait_ge(h_used, PRIMED + 2 * HB * (NG - 1) + HB)
            role = [sp.value_load(window_meta[0:1, 0, window_number(s, 0):window_number(s, 0) + 1],
                                  min_val=0, max_val=ROLES - 1) for s in (2, 3)]
            for layer in range(LAYERS):
                for s in (2, 3):
                    load(slots[s], layer, role[s - 2] * LAYERS + layer)
            load_pair(LAST_PAIR)
        LOADED = 32

        @block.gpsimd
        def _(pool):
            pool.sem_inc(window_done, PRIMED)
            pool.memset(ident[:, :], 0.0).then_inc(consts_zero, 1)
            pool.memset(ones[:, :], 1.0).then_inc(first_consts, 1)
            pool.iota(batch_id[:, :], [[1, B]], base=0, channel_multiplier=0,
                      allow_small_or_imprecise_dtypes=True).then_inc(first_consts, 1)
            pool.iota(feature_id[:, :], [[P, VB]], base=0, channel_multiplier=1,
                      allow_small_or_imprecise_dtypes=True).then_inc(first_consts, 1)
            pool.wait_ge(consts_zero, 1)
            pool.affine_select(out=ident[:, :], in_=ident[:, :], compare_op=ALU.not_equal, fill=1.0, base=0,
                               pattern=[[-1, P]], channel_multiplier=1).then_inc(first_consts, 1)
            pool.wait_ge(first_consts, FIRST_CONSTS)
            for q in range(Q):
                if q:
                    pool.wait_ge(row_ids, q)
                pool.iota(row_in_batch[quarter(q), :], [[1, 1]], base=0, channel_multiplier=1,
                          allow_small_or_imprecise_dtypes=True).then_inc(row_ids, 1)
            pool.wait_ge(row_ids, Q)
            for q in range(Q):
                if q:
                    pool.wait_ge(consts, q)
                pool.iota(slot_off[quarter(q), :], [[Q, WT]], base=q, channel_multiplier=0,
                          allow_small_or_imprecise_dtypes=True).then_inc(consts, 1)
            pool.wait_ge(consts, Q)
            pool.iota(window_id[:, :], [[1, NW]], base=0, channel_multiplier=0,
                      allow_small_or_imprecise_dtypes=True).then_inc(consts, 1)
            pool.iota(window_start8[:, :], [[WIN, WIN]], base=0, channel_multiplier=0,
                      allow_small_or_imprecise_dtypes=True).then_inc(consts, 1)
            pool.memset(minus_half[:, :], -0.5).then_inc(half_ready, 1)
            pool.wait_ge(rows_known, Q)

            def gather(g):
                for t in range(GT):
                    pool.indirect_dma_start(out=xr[:, t, :], out_offset=None, in_=x_rows,
                                            in_offset=bass.IndirectOffsetOnAxis(ap=row_idx[:, g * GT + t:g * GT + t + 1],
                                                                                axis=0)).then_inc(x_in, 16)

            def window_part(stage_name, s, layer, pair, last=False):
                slot = slots[s]
                if stage_name == "load":
                    pool.wait_ge(x1_ready, PRIMED + VB * (1 if s < 2 else NG))
                    pool.wait_ge(window_done, PRIMED + 2 * pair)
                    apart(pool)
                    pool.tensor_copy(slot.idx[:, :], out_idx[:, bass.ds(window_number(s, pair), 1), :]
                                     .rearrange("p a t -> p (a t)")).then_inc(slot.idx_ready, 1)
                if stage_name == "up":
                    pool.wait_ge(slot.var_ready, LAYERS * pair + layer + 1)
                    pool.tensor_tensor(slot.rstd[:, :], slot.var[:, :], minus_half[:, :], ALU.pow)\
                        .then_inc(slot.rstd_ready, 1)
                if stage_name == "norm":
                    if layer < LAYERS - 1:
                        pool.wait_ge(slot.loaded[layer + 1], LOADED * (pair + 1))
                        pool.wait_ge(slot.x_ready, PRIMED + LAYERS * pair + layer + 1)
                        apart(pool)
                        pool.tensor_tensor(slot.y[:, :, :], slot.x[:, :, :],
                                           slot.rows[:, layer + 1, 0, :].unsqueeze(1).to_broadcast([P, WT, V]),
                                           ALU.add).then_inc(slot.y_ready, 1)
                    if layer == LAYERS - 1:
                        pool.wait_ge(slot.idx_ready, pair + 1)
                        pool.wait_ge(slot.x_ready, PRIMED + LAYERS * (pair + 1))
                        apart(pool)
                        for t in range(WT):
                            pool.indirect_dma_start(out=out_rows, out_offset=bass.IndirectOffsetOnAxis(
                                ap=slot.idx[:, t:t + 1], axis=0), in_=slot.x[:, t, :], in_offset=None,
                                bounds_check=B * T - 1, oob_is_err=False).then_inc(slot.stored, 16)

            def stored(s, pair):
                pool.wait_ge(slots[s].stored, 16 * WT * (pair + 1))
                pool.sem_inc(window_done, 1)

            pool.wait_ge(half_ready, 1)
            gather(0)
            for g in range(1, NG - 1):
                pool.wait_ge(z_done, PRIMED + g)
                gather(g)

            def windows(pair, behind_middle=None):
                for w in PAIR:
                    window_part(*w, pair)
                    if w == ("up", 1, 0) and behind_middle:
                        behind_middle()
                for s in range(2):
                    stored(s, pair)

            def last_rows():
                pool.wait_ge(z_done, PRIMED + NG - 1)
                gather(NG - 1)
            windows(0, last_rows)
            with pool.Fori(1, LAST_PAIR) as pair:
                windows(pair)
            last_windows(window_part)
            for s, slot in enumerate(slots):
                pool.wait_ge(slot.stored, 16 * WT * (LAST_PAIR + 1 if s < 2 else 1))

        @block.scalar
        def _(act):
            for counter in (gelu_done, at_split):
                act.sem_inc(counter, PRIMED)
            for n in range(3):
                act.wait_ge(wT_turned, n + 1)
                act.activation(wT[:, n, :, :], two(bank[n][:, :]), ACT.Copy).then_inc(wT_copied, 1)
            act.wait_ge(bias_turned, 1)
            act.activation(bias[:, :], bank[6][:, 0:22], ACT.Copy).then_inc(bias_ready, 1)
            for n in range(2):
                act.wait_ge(folded, n + 1)
                act.activation(fold[:, n, :, :], two(bank[4 + n][:, :]), ACT.Copy).then_inc(fold_ready, 1)
            act.wait_ge(bias_ready, 1)

            def chunks(first, last):
                for c in range(first, last):
                    act.wait_ge(stage_in[c % STAGES], 16 * (c // STAGES + 1))
                    act.activation(high(slice(c * CHUNK, (c + 1) * CHUNK)), stage[:, c % STAGES, :], ACT.Copy)\
                        .then_inc(chunk_hi, 1)

            def attention_part(stage_name, g):
                if stage_name == "X":
                    act.wait_ge(xT_turned, g + 1)
                    apart(act)
                    for vb in range(VB):
                        act.activation(xT[:, vb, bass.ts(g, GR)], bank[4 + vb][:, :], ACT.Copy).then_inc(xT_ready, 1)
                if stage_name == "Y":
                    act.wait_ge(y_done, g + 1)
                    for vb in range(VB):
                        act.activation(yz[:, vb, :], bank[4 + vb][:, :], ACT.Copy).then_inc(y_ready, 1)
                if stage_name == "S":
                    act.wait_ge(shifted_ready, g + 1)
                    act.activation(expd[:, :, :], shifted[:, :, :], ACT.Exp, scale=float(V) ** -0.5)\
                        .then_inc(exp_ready, 1)
                if stage_name == "Z":
                    act.wait_ge(z_done, PRIMED + g + 1)
                    for vb in range(VB):
                        act.activation(yz[:, vb, :], bank[4 + vb][:, :], ACT.Copy).then_inc(z_ready, 1)
                if stage_name == "B":
                    act.wait_ge(at_done, g + 1)
                    for vb in range(VB):
                        act.activation(at_hi[:, vb, :], bank[4 + vb][:, :], ACT.Identity,
                                       bias=bias[:, BP + vb:BP + vb + 1]).then_inc(at_split, 1)

            def part(step, n, g):
                if step in ("H", "Hb"):
                    b = (CB1 if n < HB else MB1) + n % HB
                    act.wait_ge(hidden_done, 2 * HB * g + n + 1)
                    act.wait_ge(h_lo_ready, PRIMED + 2 * HB * g + max(n - 1, 0))
                    act.activation(h_full[:, n % 2, :], bank[n % 2][:, :], ACT.Gelu, bias=bias[:, b:b + 1])\
                        .then_inc(gelu_done, 1)
                    act.wait_ge(gelu_done, PRIMED + 2 * HB * g + n + 1)
                    act.wait_ge(h_used, PRIMED + 2 * HB * g + max(n - 1, 0))
                    act.activation(h_hi[:, n % 2, :], h_full[:, n % 2, :], ACT.Copy).then_inc(h_hi_ready, 1)
                if step == "C":
                    for vb in range(VB):
                        act.wait_ge(cms_copied, VB * g + vb + 1)
                        act.activation(cms_hi[:, vb, :], cms[:, vb, :], ACT.Copy).then_inc(cms_split, 1)

            def window_part(stage_name, s, layer, pair, last=False):
                slot = slots[s]
                if stage_name == "load":
                    first = act.value_load(window_meta[0:1, 1, bass.ds(window_number(s, pair), 1)], min_val=0, max_val=B - WIN)
                    act.wait_ge(x1_ready, VB * NG + PRIMED if last else VB * (pair + 1) + PRIMED)
                    apart(act)
                    act.activation(slot.xT[:, :, :], xT[:, :, bass.ds(first * T, WR)], ACT.Copy).then_inc(slot.x_in, 1)
                if stage_name == "turn" and layer > 0:
                    act.wait_ge(slot.turned, LAYERS * pair + layer + 1)
                    act.activation(slot.xT[:, :, :], two(slot.bank[:, :]), ACT.Copy).then_inc(slot.x_in, 1)
                if stage_name == "down":
                    act.wait_ge(slot.loaded[layer], LOADED * (pair + 1))
                    act.wait_ge(slot.down_done, LAYERS * pair + layer + 1)
                    act.activation(slot.h[:, :], slot.bank[:, 0:WR], ACT.Gelu, bias=slot.w[:, layer, 2 * V:2 * V + 1])\
                        .then_inc(slot.h_ready, 1)

            attention_part("X", 0)
            chunks(0, 4)
            attention_part("Y", 0)
            attention_part("S", 0)
            chunks(4, 6)
            for a in "ZB":
                attention_part(a, 0)
            chunks(6, NCHUNK)
            whole(act, part, window_part, attention_part)

        @block.vector
        def _(dve):
            for counter in (h_lo_ready, x1_ready, slots[0].x_ready, slots[1].x_ready,
                            slots[2].x_ready, slots[3].x_ready, *slots[0].layer_done, *slots[1].layer_done):
                dve.sem_inc(counter, PRIMED)
            link = linked(dve, route_step, 0)
            dve.wait_ge(meta_in, 48)
            dve.wait_ge(first_consts, FIRST_CONSTS)
            role_row, key_row, onehot, scratch = (rt[:, n, :] for n in range(4))
            role_c, code_c, key_c, rank_c, neg_c = (rc[:, n:n + 1] for n in range(5))
            link(dve.tensor_copy(code_c, code_col_i[:, :]))
            link(dve.tensor_copy(role_row, roles_i[:, :]))
            link(dve.tensor_copy(role_c, role_col_i[:, :]))
            for r, neg in ((role_row, scratch), (role_c, neg_c)):
                link(dve.tensor_scalar(neg, r, 0.0, float(ROLES), ALU.is_lt, ALU.mult))
                link(dve.tensor_tensor(r, r, neg, ALU.add))
                link(dve.tensor_scalar(r, r, 0.0, float(ROLES - 1), ALU.max, ALU.min))
            link(dve.scalar_tensor_tensor(key_row, role_row, float(B), batch_id[:, :], ALU.mult, ALU.add))
            link(dve.scalar_tensor_tensor(key_c, role_c, float(B), feature_id[0:B, 0:1], ALU.mult, ALU.add))
            link(dve.tensor_scalar(scratch[0:B, :], key_row[0:B, :], key_c, None, ALU.is_lt))
            link(dve.tensor_reduce(rank_c, scratch[0:B, :], AX.X, ALU.add))
            link(dve.tensor_scalar(onehot[0:B, :], batch_id[0:B, :], rank_c, None, ALU.is_equal))
            link(dve.tensor_scalar(pick[0:B, 0:2, :].rearrange("p a b -> p (a b)"), ones[:, :],
                                   feature_id[0:B, 0:1], None, ALU.mult))
            dve.tensor_scalar(pick[0:B, 2:4, :].rearrange("p a b -> p (a b)"), ones[:, :],
                              code_c, None, ALU.mult).then_inc(sorted_onehot, 1)
            dve.wait_ge(sorted_ids, 1)
            dve.wait_ge(row_ids, Q)
            sorted_batch, sorted_code = bank[7][:, 0:B], bank[7][:, B:2 * B]
            for q in range(Q):
                rows = slice(q * T, (q + 1) * T)
                dve.tensor_scalar(row_idx[rows, :], bank[7][rows, q:B:Q], float(T), row_in_batch[rows, :],
                                  ALU.mult, ALU.add).then_inc(rows_known, 1)
            dve.wait_ge(bias_ready, 1)
            for vb in range(VB):
                link(dve.tensor_scalar(cms_bias[:, vb, :], sorted_code, feature_id[:, vb:vb + 1],
                                       bias[:, CB2 + vb:CB2 + vb + 1], ALU.is_equal, ALU.add))
            place_row = key_row
            link(dve.tensor_scalar(place_row, sorted_batch, float(T), row_in_batch[:, :], ALU.mult, ALU.add))
            dve.wait_ge(consts, CONSTS)
            n0, n1, n2, o2, w1, w2, u1, u2 = (rs[:, n:n + 1] for n in range(8))
            for r, n in ((0, n0), (1, n1)):
                link(dve.tensor_scalar(scratch, role_row, float(r), None, ALU.is_equal))
                link(dve.tensor_reduce(n, scratch, AX.X, ALU.add))
            link(dve.tensor_tensor(o2, n0, n1, ALU.add))
            link(dve.tensor_scalar(n2, o2, -1.0, float(B), ALU.mult, ALU.add))
            for n, w in ((n0, w1), (n1, w2)):
                link(dve.tensor_scalar(scratch[:, 0:WIN], window_start8[:, :], n, None, ALU.is_lt))
                link(dve.tensor_reduce(w, scratch[:, 0:WIN], AX.X, ALU.add))
            link(dve.tensor_tensor(w2, w2, w1, ALU.add))
            link(dve.scalar_tensor_tensor(u1, w1, -float(WIN), n0, ALU.mult, ALU.add))
            link(dve.scalar_tensor_tensor(u2, w2, -float(WIN), o2, ALU.mult, ALU.add))
            link(dve.tensor_tensor(u2, u2, u1, ALU.subtract))
            in1, in2, start, end, first, role_w = (rw[:, n, 0:NW] for n in range(6))
            slot, ok, found, hit = (rw[:, n, :].rearrange("p (j t) -> p j t", t=WT) for n in range(6, 10))
            link(dve.tensor_scalar(in1, window_id[:, :], w1, None, ALU.is_ge))
            link(dve.tensor_scalar(in2, window_id[:, :], w2, None, ALU.is_ge))
            link(dve.tensor_tensor(role_w, in1, in2, ALU.add))
            link(dve.tensor_scalar(start, window_id[:, :], float(WIN), None, ALU.mult))
            link(dve.scalar_tensor_tensor(start, in1, u1, start, ALU.mult, ALU.add))
            link(dve.scalar_tensor_tensor(start, in2, u2, start, ALU.mult, ALU.add))
            link(dve.tensor_scalar(end, in1, n1, n0, ALU.mult, ALU.add))
            link(dve.scalar_tensor_tensor(end, in2, n2, end, ALU.mult, ALU.add))
            link(dve.tensor_scalar(first, start, float(B - WIN), None, ALU.min))
            link(dve.tensor_copy(window_meta[:, 0, :], role_w))
            link(dve.tensor_copy(window_meta[:, 1, :], first))
            wide = [P, NW, WT]
            link(dve.tensor_tensor(slot, first.unsqueeze(2).to_broadcast(wide),
                                   slot_off[:, :].unsqueeze(1).to_broadcast(wide), ALU.add))
            link(dve.tensor_tensor(ok, slot, start.unsqueeze(2).to_broadcast(wide), ALU.is_ge))
            link(dve.tensor_tensor(hit, slot, end.unsqueeze(2).to_broadcast(wide), ALU.is_lt))
            link(dve.tensor_tensor(ok, ok, hit, ALU.mult))
            flat = [P, NW * WT, B]
            link(dve.tensor_tensor(pick[:, :, :], rw[:, 6, :].unsqueeze(2).to_broadcast(flat),
                                   batch_id[:, :].unsqueeze(1).to_broadcast(flat), ALU.is_equal))
            link(dve.tensor_tensor(pick[:, :, :], pick[:, :, :], place_row.unsqueeze(1).to_broadcast(flat), ALU.mult))
            link(dve.tensor_reduce(rw[:, 8, :], pick[:, :, :], AX.X, ALU.add))
            link(dve.scalar_tensor_tensor(found, ok, -float(OUT_OF_RANGE), found, ALU.mult, ALU.add))
            dve.tensor_scalar(out_idx[:, :, :], found, float(OUT_OF_RANGE), None, ALU.add).then_inc(windows_known, 1)
            dve.memset(pd[:, :, :], 0.0).then_inc(pd_clear, 1)
            dve.sem_inc(prepared, 1)

            def chunks(first, last):
                for c in range(first, last):
                    cols = slice(c * CHUNK, (c + 1) * CHUNK)
                    dve.wait_ge(chunk_hi, c + 1)
                    dve.tensor_tensor(low(cols), stage[:, c % STAGES, :], high(cols).bitcast(F32),
                                      ALU.subtract).then_inc(chunk_lo, 1)

            def attention_part(stage_name, g):
                if stage_name == "S":
                    link = linked(dve, softmax_step, SOFTMAX_STEPS * g)
                    dve.wait_ge(scores_done, g + 1)
                    own = [bank[4][quarter(q), :].rearrange("p (i c) -> p i c", c=P)[:, :, quarter(q)]
                           for q in range(Q)]
                    for q in range(Q):
                        ins = dve.tensor_reduce(row_max[quarter(q), :], own[q], AX.X, ALU.max)
                    link(ins)
                    for q in range(Q):
                        ins = dve.tensor_tensor(shifted[quarter(q), :, :], own[q],
                                                row_max[quarter(q), :].unsqueeze(2).to_broadcast([T, GT, T]),
                                                ALU.subtract)
                    ins.then_inc(shifted_ready, 1)
                if stage_name == "P":
                    link = linked(dve, softmax_step, SOFTMAX_STEPS * g + 1)
                    dve.wait_ge(exp_ready, g + 1)
                    link(dve.tensor_reduce(row_sum[:, 0, :], expd[:, :, :], AX.X, ALU.add))
                    link(dve.reciprocal(row_sum[:, 1, :], row_sum[:, 0, :]))
                    link(dve.tensor_tensor(prob[:, :, :], expd[:, :, :],
                                           row_sum[:, 1, :].unsqueeze(2).to_broadcast([P, GT, T]), ALU.mult))
                    link(dve.transpose(probT[:, :, :], prob[:, :, :]))
                    for q in range(Q):
                        ins = dve.tensor_copy(pd[quarter(q), :, quarter(q)], probT[quarter(q), :, :])
                    ins.then_inc(pd_ready, 1)
                if stage_name == "B":
                    for vb in range(VB):
                        dve.wait_ge(at_split, PRIMED + 2 * VB * g + VB)
                        dve.scalar_tensor_tensor(at_lo[:, vb, :], bank[4 + vb][:, :], bias[:, BP + vb:BP + vb + 1],
                                                 at_hi[:, vb, :].bitcast(F32), ALU.add, ALU.subtract)\
                            .then_inc(at_split, 1)

            def part(step, n, g):
                if step in ("H", "Hb"):
                    dve.wait_ge(h_hi_ready, 2 * HB * g + n + 1)
                    dve.tensor_tensor(h_lo[:, n % 2, :], h_full[:, n % 2, :], h_hi[:, n % 2, :].bitcast(F32),
                                      ALU.subtract).then_inc(h_lo_ready, 1)
                if step == "C":
                    dve.wait_ge(h_used, PRIMED + 2 * HB * g + HB)
                    for vb in range(VB):
                        dve.tensor_tensor(
                            cms[:, vb, :].rearrange("p (b t) -> p b t", t=T),
                            bank[2 + vb][:, :].rearrange("p (b t) -> p b t", t=T),
                            cms_bias[:, vb, bass.ts(g, GB)].unsqueeze(2).to_broadcast([P, GB, T]), ALU.add)\
                            .then_inc(cms_copied, 1)
                    for vb in range(VB):
                        dve.wait_ge(cms_split, 2 * VB * g + VB)
                        dve.tensor_tensor(cms_lo[:, vb, :], cms[:, vb, :], cms_hi[:, vb, :].bitcast(F32),
                                          ALU.subtract).then_inc(cms_split, 1)
                    for vb in range(VB):
                        dve.tensor_tensor(xT[:, vb, bass.ts(g, GR)], xT[:, vb, bass.ts(g, GR)], cms[:, vb, :],
                                          ALU.add).then_inc(base_ready, 1)
                if step == "F":
                    dve.wait_ge(h_used, PRIMED + 2 * HB * (g + 1))
                    dve.wait_ge(base_ready, VB * (g + 1))
                    for vb in range(VB):
                        dve.scalar_tensor_tensor(cms[:, vb, :], bank[2 + vb][:, :], bias[:, MB2 + vb:MB2 + vb + 1],
                                                 xT[:, vb, bass.ts(g, GR)], ALU.add, ALU.add).then_inc(mod_summed, 1)
                    for vb in range(VB):
                        dve.wait_ge(mod_summed, VB * g + vb + 1)
                        dve.tensor_scalar(xT[:, vb, bass.ts(g, GR)], cms[:, vb, :], 0.0, 1.0, ALU.max, ALU.min)\
                            .then_inc(x1_ready, 1)

            def window_part(stage_name, s, layer, pair, last=False):
                slot = slots[s]

                def row(n, lay):
                    return slot.rows[:, lay, n, :].unsqueeze(1).to_broadcast([P, WT, V])
                if stage_name == "turn" and layer == 0:
                    dve.wait_ge(slot.loaded[0], LOADED * (pair + 1))
                    dve.wait_ge(slot.turned, LAYERS * pair + 1)
                    dve.tensor_tensor(slot.y[:, :, :], two((slot.sum_bank if last else slot.bank)[:, :]), row(0, 0),
                                      ALU.add)\
                        .then_inc(slot.y_ready, 1)
                if stage_name == "up":
                    link = linked(dve, slot.norm_step, NORM_STEPS * (LAYERS * pair + layer) + (1 if last else 0))
                    if layer < LAYERS - 1:
                        dve.wait_ge(slot.loaded[layer + 1], LOADED * (pair + 1))
                    dve.wait_ge(slot.up_done, LAYERS * pair + layer + 1)
                    dve.wait_ge(slot.y_ready, LAYERS * pair + layer + 1)
                    if last:
                        summed = two(slot.sum_bank[:, :])
                        dve.sem_inc(slot.norm_step, 1)
                    else:
                        summed = slot.y
                        link(dve.tensor_tensor(slot.y[:, :, :], two(slot.bank[:, :]), slot.y[:, :, :], ALU.add))
                    for t in range(WT):
                        ins = dve.bn_stats(slot.stats[:, t, :], summed[:, t, :])
                    link(ins)
                    apart(dve)
                    for t in range(WT):
                        ins = dve.bn_aggr(slot.moments[:, t, :], slot.stats[:, t, :])
                    link(ins)
                    dve.tensor_scalar(slot.var[:, :], slot.moments[:, :, 1:2].rearrange("p t a -> p (t a)"), EPS, None,
                                      ALU.add).then_inc(slot.var_ready, 1)
                    for t in range(WT):
                        ins = dve.scalar_tensor_tensor(slot.y[:, t, :], summed[:, t, :], slot.moments[:, t, 0:1],
                                                       slot.rows[:, layer, 1, :], ALU.subtract, ALU.mult)
                    link(ins)
                if stage_name == "norm":
                    dve.wait_ge(slot.norm_step, NORM_STEPS * (LAYERS * pair + layer + 1))
                    dve.wait_ge(slot.rstd_ready, LAYERS * pair + layer + 1)
                    for t in range(WT):
                        ins = dve.scalar_tensor_tensor(slot.x[:, t, :], slot.y[:, t, :], slot.rstd[:, t:t + 1],
                                                       slot.rows[:, layer, 2, :], ALU.mult, ALU.add)
                    ins.then_inc(slot.x_ready, 1)
                    if s < 2:
                        dve.wait_ge(slot.x_ready, PRIMED + LAYERS * pair + layer + 1)
                        dve.sem_inc(slot.layer_done[layer], 1)

            chunks(0, 4)
            dve.wait_ge(pd_clear, 1)
            attention_part("S", 0)
            attention_part("P", 0)
            chunks(4, 6)
            attention_part("B", 0)
            chunks(6, NCHUNK)
            whole(dve, part, window_part, attention_part)

        @block.tensor
        def _(pe):
            for counter in (z_done, h_used):
                pe.sem_inc(counter, PRIMED)
            pe.wait_ge(sorted_onehot, 1)
            for n in range(2):
                ins = pe.matmul(bank[7][:, n * B:(n + 1) * B], pick[0:B, 2 * n:2 * n + 2, :].rearrange("p a b -> p (a b)"),
                                rt[0:B, 2, :], start=True, stop=True)
            ins.then_inc(sorted_ids, 1)
            pe.wait_ge(first_consts, FIRST_CONSTS)
            pe.wait_ge(raw_in, 16 * 4)
            for n in range(3):
                for eb in range(VB):
                    for db in range(VB):
                        ins = pe.transpose(bank[n][:, eb * V + db * P:eb * V + (db + 1) * P],
                                           raw[:, n, db, eb * P:(eb + 1) * P], ident[:, :])
                ins.then_inc(wT_turned, 1)
            pe.wait_ge(bias_in, 16 * 5)
            pe.transpose(bank[6][:, 0:22], bias_rows[:, :], ident[0:22, 0:22]).then_inc(bias_turned, 1)
            for n, (lhs, rhs) in enumerate(((wT[:, 0], wT[:, 1]), (wT[:, 2], raw[:, 3]))):
                pe.wait_ge(wT_copied, 2 + n)
                for db in range(VB):
                    for eb in range(VB):
                        ins = pe.matmul(bank[4 + n][:, db * V:(db + 1) * V], lhs[:, eb, db * P:(db + 1) * P],
                                        rhs[:, eb, :], start=(eb == 0), stop=(eb == VB - 1))
                ins.then_inc(folded, 1)
            pe.wait_ge(fold_ready, 2)

            def attention_part(stage_name, g):
                first = g * GR
                if stage_name == "X":
                    pe.wait_ge(x_in, 16 * GT * (g + 1))
                    pe.wait_ge(at_split, PRIMED + 2 * VB * g)
                    for vb in range(VB):
                        for i in range(GT):
                            ins = pe.transpose(bank[4 + vb][:, i * P:(i + 1) * P], xr[:, i, vb * P:(vb + 1) * P],
                                               ident[:, :])
                    ins.then_inc(xT_turned, 1)
                if stage_name == "Y":
                    pe.wait_ge(xT_ready, VB * (g + 1))
                    for ob in range(VB):
                        for k in range(VB):
                            ins = pe.matmul(bank[4 + ob][:, :], fold[:, 0, k, ob * P:(ob + 1) * P],
                                            xT[:, k, bass.ds(first, GR)], start=(k == 0), stop=(k == VB - 1))
                    ins.then_inc(y_done, 1)
                if stage_name == "S":
                    pe.wait_ge(y_ready, VB * (g + 1))
                    for i in range(GT):
                        cols = slice(i * P, (i + 1) * P)
                        for k in range(VB):
                            ins = pe.matmul(bank[4][:, cols], yz[:, k, cols], xT[:, k, bass.ds(first + i * P, P)],
                                            start=(k == 0), stop=(k == VB - 1))
                    ins.then_inc(scores_done, 1)
                if stage_name == "Z":
                    pe.wait_ge(pd_ready, g + 1)
                    for vb in range(VB):
                        for i in range(GT):
                            ins = pe.matmul(bank[4 + vb][:, i * P:(i + 1) * P], xr[:, i, vb * P:(vb + 1) * P],
                                            pd[:, i, :], start=True, stop=True)
                    ins.then_inc(z_done, 1)
                if stage_name == "A":
                    pe.wait_ge(z_ready, VB * (g + 1))
                    for ob in range(VB):
                        for k in range(VB):
                            ins = pe.matmul(bank[4 + ob][:, :], fold[:, 1, k, ob * P:(ob + 1) * P], yz[:, k, :],
                                            start=(k == 0), stop=(k == VB - 1))
                    ins.then_inc(at_done, 1)

            def part(step, n, g):
                if step in ("H", "Ha", "Hb"):
                    w, j = (CW1, n) if n < HB else (MW1, n - HB)
                    k_all = VB if n < HB else 2 * VB
                    ks = range(VB) if step == "Ha" else range(VB, 2 * VB) if step == "Hb" else range(k_all)
                    if step != "Hb":
                        pe.wait_ge(gelu_done, PRIMED + 2 * HB * g + max(n - 1, 0))
                    if n == 0:
                        pe.wait_ge(at_split, PRIMED + 2 * VB * (g + 1))
                    if isinstance(g, int) and g == 0 and n in (0, HB):
                        pe.wait_ge(chunk_lo, 2 if n == 0 else 8)
                    if n == HB and step == "Hb":
                        pe.wait_ge(cms_split, 2 * VB * g + VB)
                        for k in ks:
                            cols = slice(w + k * H, w + k * H + P)
                            pe.matmul(bank[0][:, :], high(cols), cms_hi[:, k - VB, :], start=False, stop=False)
                            pe.matmul(bank[0][:, :], low(cols), cms_hi[:, k - VB, :], start=False, stop=False)
                        pe.wait_ge(cms_split, 2 * VB * (g + 1))
                        for k in ks:
                            ins = pe.matmul(bank[0][:, :], high(slice(w + k * H, w + k * H + P)), cms_lo[:, k - VB, :],
                                            start=False, stop=(k == k_all - 1))
                        ins.then_inc(hidden_done, 1)
                        return
                    for k in ks:
                        cols = slice(w + k * H + j * P, w + k * H + (j + 1) * P)
                        r_hi, r_lo = ((at_hi[:, k, :], at_lo[:, k, :]) if k < VB
                                      else (cms_hi[:, k - VB, :], cms_lo[:, k - VB, :]))
                        ins = mm3(pe, bank[n % 2][:, :], high(cols), low(cols), r_hi, r_lo,
                                  k == 0, k == k_all - 1)
                    if step != "Ha":
                        ins.then_inc(hidden_done, 1)
                if step == "D":
                    w, j = (CW2, n) if n < HB else (MW2, n - HB)
                    pe.wait_ge(h_hi_ready, 2 * HB * g + n + 1)
                    if n == 0 and not (isinstance(g, int) and g == 0):
                        pe.wait_ge(mod_summed, VB * g)
                    if isinstance(g, int) and g == 0 and n in (0, HB):
                        pe.wait_ge(chunk_lo, 4 if n == 0 else NCHUNK)
                    for ob in range(VB):
                        cols = slice(w + j * V + ob * P, w + j * V + (ob + 1) * P)
                        pe.matmul(bank[2 + ob][:, :], high(cols), h_hi[:, n % 2, :], start=(j == 0), stop=False)
                        pe.matmul(bank[2 + ob][:, :], low(cols), h_hi[:, n % 2, :], start=False, stop=False)
                    pe.wait_ge(h_lo_ready, PRIMED + 2 * HB * g + n + 1)
                    for ob in range(VB):
                        cols = slice(w + j * V + ob * P, w + j * V + (ob + 1) * P)
                        ins = pe.matmul(bank[2 + ob][:, :], high(cols), h_lo[:, n % 2, :], start=False,
                                        stop=(j == HB - 1))
                    ins.then_inc(h_used, 1)

            def window_part(stage_name, s, layer, pair, last=False):
                slot = slots[s]
                if stage_name == "turn" and layer == 0:
                    pe.wait_ge(slot.x_in, LAYERS * pair + 1)
                    if not last:
                        pe.wait_ge(slot.x_ready, PRIMED + LAYERS * pair)
                    for t in range(WT):
                        for vb in range(VB):
                            ins = pe.transpose((slot.sum_bank if last else slot.bank)[:, t * V + vb * P:t * V + (vb + 1) * P],
                                               slot.xT[:, vb, t * P:(t + 1) * P], ident[:, :])
                    ins.then_inc(slot.turned, 1)
                if stage_name == "turn" and layer > 0:
                    pe.wait_ge(slot.x_ready, PRIMED + LAYERS * pair + layer)
                    for vb in range(VB):
                        for t in range(WT):
                            ins = pe.transpose(slot.bank[:, vb * WR + t * P:vb * WR + (t + 1) * P],
                                               slot.x[:, t, vb * P:(vb + 1) * P], ident[:, :])
                    ins.then_inc(slot.turned, 1)
                if stage_name == "down":
                    pe.wait_ge(slot.loaded[layer], LOADED * (pair + 1))
                    if layer == 0 and last:
                        pe.wait_ge(slot.x_ready, PRIMED + LAYERS * pair)
                    elif layer == 0:
                        pe.wait_ge(slot.y_ready, LAYERS * pair + 1)
                    pe.wait_ge(slot.x_in, LAYERS * pair + layer + 1)
                    for vb in range(VB):
                        ins = pe.matmul(slot.bank[:, 0:WR], slot.w[:, layer, vb * KD:(vb + 1) * KD], slot.xT[:, vb, :],
                                        start=(vb == 0), stop=(vb == VB - 1))
                    ins.then_inc(slot.down_done, 1)
                if stage_name == "up":
                    up_bank = slot.sum_bank if last else slot.bank
                    if last:
                        pe.wait_ge(slot.y_ready, LAYERS * pair + layer + 1)
                        pe.matmul(up_bank[:, :], ident[:, :], slot.y[:, :, :].rearrange("p t v -> p (t v)"),
                                  start=True, stop=False)
                    pe.wait_ge(slot.h_ready, LAYERS * pair + layer + 1)
                    for t in range(WT):
                        ins = pe.matmul(up_bank[:, t * V:(t + 1) * V], slot.h[:, t * P:(t + 1) * P],
                                        slot.w[:, layer, V:2 * V], start=not last, stop=not last or t == WT - 1)
                    ins.then_inc(slot.up_done, 1)

            for a in "XYSZA":
                attention_part(a, 0)
            whole(pe, part, window_part, attention_part)


_ADAPTER = [("W_down", "b_down", "W_up", "b_up", "gamma", "beta"),
            ("W_down", "b_down", "W_up", "b_up", "ln_w", "ln_b"),
            ("W_down", "b_down", "W_up", "b_up", "ln_w", "ln_b")]
_INS = ["x", "itok_B_17_1546", "itok_B_1_2"] + ["L0_cond_" + n for n in (
    "Wq", "Wk", "Wv", "Wp", "bp", "cW1", "cb1", "cW2", "cb2", "mW1", "mb1", "mW2", "mb2")]
_INS_ADAPTERS = [[f"L{i + 1}_cond_{n}" for n in names] for i, names in enumerate(_ADAPTER)]


def kernel(**inputs):
    import numpy as _np
    import concourse.bacc as _bacc
    from concourse import mybir as _mybir
    from concourse.bass_utils import run_bass_kernel_spmd as _run

    nc = _bacc.Bacc("TRN2", target_bir_lowering=False, num_devices=1)
    arrays = {}

    def declare(name):
        a = _np.ascontiguousarray(inputs[name])
        arrays[f"in_{name}"] = a
        return nc.dram_tensor(f"in_{name}", a.shape, _mybir.dt.from_np(a.dtype), kind="ExternalInput").ap()

    args = [declare(n) for n in _INS]
    adapters = [[declare(n) for n in names] for names in _INS_ADAPTERS]
    out = nc.dram_tensor("out_0", (64, 32, 256), _mybir.dt.float32, kind="ExternalOutput").ap()
    build(nc, *args, adapters, out)
    r = _run(nc, [arrays], core_ids=[0])
    return r.results[0]["out_0"]
```
